# Optimizing a Trainium2 kernel written in Bass

```python
import numpy as np
import jax
import jax.numpy as jnp

def _softmax(x, axis=-1):
    return jax.nn.softmax(x, axis=axis)

def _gelu(x):
    return jax.nn.gelu(x, approximate=True)

def _silu(x):
    return jax.nn.silu(x)

def _sigmoid(x):
    return jax.nn.sigmoid(x)

def _layernorm(x, axis=-1, eps=1e-05):
    m = jnp.mean(x, axis=axis, keepdims=True)
    v = jnp.var(x, axis=axis, keepdims=True)
    return (x - m) / jnp.sqrt(v + eps)

def _scatter_add(tgt, idx, src, axis=0):
    return tgt.at[idx].add(src)

def _segment_sum(src, seg, n):
    return jax.ops.segment_sum(src, seg, n)
kernel_name = 'mk_adj_resnorm_d1_adj_r2_be6616'

def setup_inputs(seed: int=0):
    np.random.seed(seed)
    _w = jnp.asarray

    def _rec_inputs():
        import jax
        import jax.numpy as jnp
        _gk = jax.random.key(seed)
        x = -0.0002928 + 1 * jax.random.normal(jax.random.fold_in(_gk, 1), (8, 1024, 128), jnp.float32)
        _w = (1.0 + jnp.arange(1024, dtype=jnp.float32)) ** (-0.5)
        _w = _w / _w.mean()
        _pij = jnp.clip(0.0078125 * _w[:, None] * _w[None, :], 0.0, 1.0)
        _a = jax.random.uniform(jax.random.fold_in(_gk, 2), (8, 1024, 1024)) < _pij
        adj = _a.astype(jnp.int32)
        return (x, adj)
    x, adj = _rec_inputs()

    def _L0_gnn_setup():
        import jax, jax.numpy as jnp
        import numpy as np
        LEAKY_SLOPE = 0.2
        NEG_INF = -9000000000000000.0

        def _edge_scores(h, a_k):
            e = jnp.einsum('bid,bjd->bij', h * a_k[:, 0], h)
            return jax.nn.leaky_relu(e, negative_slope=LEAKY_SLOPE)
        key = jax.random.key(seed)
        k1, k2, k3, k4, k5, k6 = jax.random.split(key, 6)
        B, N, D = (32, 256, 128)
        hidden = jax.random.normal(k1, (B, N, D), dtype=jnp.float32)
        adj = jax.random.randint(k2, (B, N, N), 0, 5, dtype=jnp.int32)
        a_0 = jax.random.normal(k3, (D, 1), dtype=jnp.float32)
        a_1 = jax.random.normal(k4, (D, 1), dtype=jnp.float32)
        a_2 = jax.random.normal(k5, (D, 1), dtype=jnp.float32)
        a_3 = jax.random.normal(k6, (D, 1), dtype=jnp.float32)
        return {'hidden': hidden, 'adj': adj, 'a_0': a_0, 'a_1': a_1, 'a_2': a_2, 'a_3': a_3}
    _L0_gnn_all = _L0_gnn_setup()
    _L0_gnn_in = {k: v for k, v in _L0_gnn_all.items() if k in ('a_0', 'a_1', 'a_2', 'a_3')}
    del _L0_gnn_all
    return {'x': x, 'adj': adj, 'L0_gnn_a_0': _L0_gnn_in['a_0'], 'L0_gnn_a_1': _L0_gnn_in['a_1'], 'L0_gnn_a_2': _L0_gnn_in['a_2'], 'L0_gnn_a_3': _L0_gnn_in['a_3']}

def reference(x, adj, L0_gnn_a_0, L0_gnn_a_1, L0_gnn_a_2, L0_gnn_a_3):
    import jax
    import jax.numpy as jnp

    def _L0_gnn_ref(hidden, adj, a_0, a_1, a_2, a_3):
        import jax, jax.numpy as jnp
        import numpy as np
        LEAKY_SLOPE = 0.2
        NEG_INF = -9000000000000000.0

        def _edge_scores(h, a_k):
            e = jnp.einsum('bid,bjd->bij', h * a_k[:, 0], h)
            return jax.nn.leaky_relu(e, negative_slope=LEAKY_SLOPE)
        h = hidden
        e_0 = _edge_scores(h, a_0)
        e_1 = _edge_scores(h, a_1)
        e_2 = _edge_scores(h, a_2)
        e_3 = _edge_scores(h, a_3)
        scores = jnp.where(adj == 1, e_0, NEG_INF)
        scores = jnp.where(adj == 2, e_1, scores)
        scores = jnp.where(adj == 3, e_2, scores)
        scores = jnp.where(adj == 4, e_3, scores)
        alpha = jax.nn.softmax(scores, axis=-1)
        return jnp.einsum('bij,bjd->bid', alpha, h)
    x = _layernorm(x + _L0_gnn_ref(x, adj, L0_gnn_a_0, L0_gnn_a_1, L0_gnn_a_2, L0_gnn_a_3), axis=-1)
    return x

_drawn_inputs = setup_inputs


def setup_inputs(seed=0):
    import zlib

    import numpy as np

    out = dict(_drawn_inputs(seed))
    spreads = {}
    factors = {}
    for name, (base, spread) in spreads.items():
        noise = np.random.default_rng([zlib.crc32(name.encode()), seed]).standard_normal(out[name].shape)
        drawn = base * np.exp(spread * noise) if base else spread * noise
        out[name] = jnp.asarray(drawn.astype(out[name].dtype))
    for name, factor in factors.items():
        out[name] = (out[name] * factor).astype(out[name].dtype)
    return out
```

```python
from contextlib import ExitStack

import concourse.bass as bass
from concourse import mybir

ALU = mybir.AluOpType
ACT = mybir.ActivationFunctionType
AX = mybir.AxisListType
F32 = mybir.dt.float32
F32R = mybir.dt.float32r
I32 = mybir.dt.int32

P = 128
SLOPE = 0.2
BIG = 2.0 ** 90
EPS = 1e-5
HALF = 512
PERIOD = 16


def gat_residual_norm(nc, x, adj, a_0, a_1, a_2, a_3, out):
    B, N, D = x.shape
    TB = N // P
    T = B * TB
    G = HALF // P
    NG = T // G
    BATCHES, GROUPS = PERIOD // TB, PERIOD // G
    assert D == P and N == 2 * HALF and T % PERIOD == 0 and PERIOD == 2 * TB
    FIRST = TB
    LAST = T - TB
    MIX, BACK = 6, 11
    END = G * (NG - 1) + BACK + 1
    OLD = TB - 1
    RA, RM = 8, 4

    with ExitStack() as ctx:
        def sb(name, shape, dt=F32):
            return ctx.enter_context(nc.sbuf_tensor(name, shape, dt))

        def psum(name, shape):
            return ctx.enter_context(nc.psum_tensor(name, shape, F32))

        def sem(name):
            return ctx.enter_context(nc.semaphore(name))

        adj_sb = sb("adj_sb", [P, RA, N], I32)
        mask = sb("mask", [P, RM, N])
        leaky = sb("leaky", [P, P * TB * (TB + 1) // 2])
        masked = sb("masked", [P, 2, N])
        probs = sb("probs", [P, 2, N])
        probsT = sb("probsT", [P, 2, TB, HALF])
        h_hi = sb("h_hi", [P, 2, N], F32R)
        h_lo = sb("h_lo", [P, 2, N], F32R)
        u_hi = sb("u_hi", [P, 2, N], F32R)
        u_lo = sb("u_lo", [P, 2, N], F32R)
        hT = sb("hT", [P, N])
        uT = sb("uT", [P, N])
        x_turn = sb("x_turn", [P, TB, D])
        x_sb = sb("x_sb", [P, 2, TB, D])
        mixT = sb("mixT", [P, HALF])
        y = sb("y", [P, 2, G, D])
        normed = sb("normed", [P, 2, G, D])
        ident = sb("ident", [P, P])
        a_sb = sb("a_sb", [P, 4])
        minus_half = sb("minus_half", [P, G])
        negmax = sb("negmax", [P, PERIOD])
        oldmin = sb("oldmin", [P, 2])
        rowsum = sb("rowsum", [P, PERIOD])
        rinv = sb("rinv", [P, G])
        stats = sb("stats", [P, G, 6])
        moments = sb("moments", [P, 2, G, 2])
        rstd = sb("rstd", [P, G])
        negmean = sb("negmean", [P, G])
        lifted = sb("lifted", [P, TB])
        uniform = sb("uniform", [P, TB])
        uneven = sb("uneven", [P, TB])
        odd = sb("odd", [P, TB])
        warm = sb("warm", [P, 1])
        ones = sb("ones", [P, 1])
        odd_rows = sb("odd_rows", [P, 1])
        verdict = sb("verdict", [1, 1], I32)

        S = psum("S", [P, 2, N])
        turned = psum("turned", [P, 2, HALF])
        mix = psum("mix", [P, HALF])
        aux = psum("aux", [P, HALF])

        adj_loaded = [sem(f"adj_loaded{i}") for i in range(RA // 2)]
        a_loaded = sem("a_loaded")
        x_turn_loaded = sem("x_turn_loaded")
        x_loaded = [sem(f"x_loaded{i}") for i in range(2)]
        stored = sem("stored")
        consts_ready = sem("consts_ready")
        consts_step = sem("consts_step")
        mask_ready = sem("mask_ready")
        xT_ready = sem("xT_ready")
        hT_ready = sem("hT_ready")
        u_ready = sem("u_ready")
        split_part = sem("split_part")
        split_ready = sem("split_ready")
        S_ready = sem("S_ready")
        copied = sem("copied")
        leaky_ready = sem("leaky_ready")
        old_masked = sem("old_masked")
        masked_ready = sem("masked_ready")
        probs_ready = sem("probs_ready")
        turned_ready = sem("turned_ready")
        probsT_ready = sem("probsT_ready")
        mix_step = sem("mix_step")
        mixT_ready = sem("mixT_ready")
        back_ready = sem("back_ready")
        rinv_ready = sem("rinv_ready")
        y_ready = sem("y_ready")
        stats_ready = sem("stats_ready")
        moments_ready = sem("moments_ready")
        norm_step = sem("norm_step")
        normed_ready = sem("normed_ready")
        normed_free = sem("normed_free")
        odd_step = sem("odd_step")
        odd_ready = sem("odd_ready")
        counted = sem("counted")
        verdict_ready = sem("verdict_ready")
        dve_turn = sem("dve_turn")
        pool_turn = sem("pool_turn")
        sp_turn = sem("sp_turn")

        g_loaded = sem("g_loaded")
        g_x_loaded = sem("g_x_loaded")
        g_xT_ready = sem("g_xT_ready")
        g_hT_ready = sem("g_hT_ready")
        g_rowsT_ready = sem("g_rowsT_ready")
        g_u_ready = sem("g_u_ready")
        g_S_ready = sem("g_S_ready")
        g_edges_ready = sem("g_edges_ready")
        g_cand_ready = sem("g_cand_ready")
        g_best_ready = sem("g_best_ready")
        g_leaky_ready = sem("g_leaky_ready")
        g_max_ready = sem("g_max_ready")
        g_probs_ready = sem("g_probs_ready")
        g_turned_ready = sem("g_turned_ready")
        g_probsT_ready = sem("g_probsT_ready")
        g_mixed = sem("g_mixed")
        g_rinv_ready = sem("g_rinv_ready")
        g_y_ready = sem("g_y_ready")
        g_stats_ready = sem("g_stats_ready")
        g_moments_ready = sem("g_moments_ready")
        g_norm_step = sem("g_norm_step")
        g_normed_ready = sem("g_normed_ready")
        g_stored = sem("g_stored")
        g_done = sem("g_done")
        g_turn = {e: sem(f"g_turn_{e}") for e in ("sp", "pool", "dve", "pe")}

        def due(r, per_period, count):
            return count if isinstance(r, int) else r * per_period + count

        START = 2

        def index(r, per_period, n):
            return n if isinstance(r, int) else r * per_period + n

        def steps(eng, step):
            for s in range(0, FIRST):
                step(0, s)
            with eng.Fori(0, (LAST - FIRST) // PERIOD) as r:
                for s in range(FIRST, FIRST + PERIOD):
                    step(r, s)
            for s in range(LAST, END):
                step(0, s)

        def own_turn(eng, r, turns):
            if not isinstance(r, int):
                eng.sem_inc(turns, 1)

        def leaky_cols(J, c0, c1):
            at = P * (TB * J - J * (J - 1) // 2) - P * J
            return leaky[:, at + c0:at + c1]

        out_g = out.rearrange("b (g k p) d -> (b g) p k d", k=G, p=P)
        adj_p = adj.rearrange("b (q k p) n -> (b q) p k n", k=2, p=P)
        x_b = x.rearrange("b (t p) d -> b p t d", p=P)

        R = 4
        g_rows, g_u, g_best = y[:, 1, 0], uT[:, 0:R * P], probs[:, 0]
        g_probsT = probsT[:, 0, :, 0:P]
        out_t = out.rearrange("b (t p) d -> (b t) p d", p=P)
        x_t = x.rearrange("b (t p) d -> (b t) p d", p=P)
        adj_t = adj.rearrange("b (t p) n -> (b t) p n", p=P)

        def general(eng, per_batch, per_tile):
            eng.wait_ge(verdict_ready, 1)
            rows = eng.value_load(verdict[0:1, 0:1])
            with eng.If(rows > 0):
                with eng.Fori(0, B) as b:
                    if per_batch:
                        per_batch(b)
                    with eng.Fori(0, TB) as t:
                        per_tile(b * TB + t)

        block = ctx.enter_context(nc.Block())

        @block.sync
        def _(sp):
            sp.dma_start(x_turn[:], x_b[0]).then_inc(x_turn_loaded, 16)
            sp.dma_start(adj_sb[:, 0:2, :], adj_p[0]).then_inc(adj_loaded[0], 16)
            for k, a in enumerate((a_0, a_1, a_2, a_3)):
                sp.dma_start(a_sb[:, k:k + 1], a).then_inc(a_loaded, 16)
            sp.dma_start(x_sb[:, 0], x_b[0]).then_inc(x_loaded[0], 16)
            for q in range(1, RA // 2):
                sp.dma_start(adj_sb[:, 2 * q:2 * q + 2, :], adj_p[q]).then_inc(adj_loaded[q], 16)

            def step(r, s):
                n = s // TB + 1
                if s % TB == 0 and n < B:
                    sp.wait_ge(xT_ready, due(r, 2 * BATCHES, 2 * n))
                    own_turn(sp, r, sp_turn)
                    sp.dma_start(x_turn[:], x_b[index(r, BATCHES, n)]).then_inc(x_turn_loaded, 16)
                if s % 2 == 0 and s + RA < T:
                    sp.wait_ge(mask_ready, due(r, PERIOD, s + 2))
                    own_turn(sp, r, sp_turn)
                    q = (s + RA) // 2
                    sp.dma_start(adj_sb[:, s % RA:s % RA + 2, :], adj_p[index(r, PERIOD // 2, q)]) \
                        .then_inc(adj_loaded[q % (RA // 2)], 16)
                if s % TB == TB - 1 and n < B:
                    if s > TB:
                        sp.wait_ge(y_ready, due(r, GROUPS, START + 2 * (n - 1)))
                        own_turn(sp, r, sp_turn)
                    sp.dma_start(x_sb[:, n % 2], x_b[index(r, BATCHES, n)]).then_inc(x_loaded[n % 2], 16)
                g = (s - BACK) // G
                if (s - BACK) % G == 0 and g >= 0:
                    sp.wait_ge(normed_ready, due(r, GROUPS, START + g + 1))
                    own_turn(sp, r, sp_turn)
                    sp.dma_start(out_g[index(r, GROUPS, g)], normed[:, g % 2]).then_inc(stored, 16)
                    sp.wait_ge(stored, due(r, 16 * GROUPS, 16 * (g + 1)))
                    sp.sem_inc(normed_free, 1)

            sp.sem_inc(normed_free, START)
            steps(sp, step)

            def load_x(b):
                sp.wait_ge(g_done, b * TB + 1)
                sp.sem_inc(g_turn["sp"], 1)
                sp.dma_start(x_sb[:, 0], x_b[b]).then_inc(g_x_loaded, 16)

            def tile(n):
                sp.wait_ge(g_done, n + 1)
                sp.sem_inc(g_turn["sp"], 1)
                sp.dma_start(adj_sb[:, 0], adj_t[n]).then_inc(g_loaded, 16)
                sp.dma_start(g_rows, x_t[n]).then_inc(g_loaded, 16)
                sp.wait_ge(g_normed_ready, n + 1)
                sp.sem_inc(g_turn["sp"], 1)
                sp.dma_start(out_t[n], normed[:, 0, 0]).then_inc(g_stored, 16)
                sp.wait_ge(g_stored, n * 16 + 16)
                sp.sem_inc(g_done, 1)

            sp.sem_inc(g_done, 1)
            general(sp, load_x, tile)

        @block.gpsimd
        def _(pool):
            nc.gpsimd.memset(ident[:], 0.0).then_inc(consts_step, 1)
            nc.gpsimd.memset(minus_half[:], -0.5)
            nc.gpsimd.memset(ones[:], 1.0)
            nc.gpsimd.memset(odd[:], 0.0)
            pool.wait_ge(consts_step, 1)
            nc.gpsimd.affine_select(out=ident[:], in_=ident[:], compare_op=ALU.not_equal, fill=1.0, base=0,
                                    pattern=[[-1, P]], channel_multiplier=1).then_inc(consts_ready, 1)

            def make_mask(r, t):
                pool.wait_ge(adj_loaded[t // 2 % (RA // 2)], due(r, 16 * PERIOD // RA, 16 * (t // RA + 1)))
                if t >= RM:
                    pool.wait_ge(masked_ready, due(r, PERIOD, t - RM + 1))
                own_turn(pool, r, pool_turn)
                nc.gpsimd.tensor_scalar(mask[:, t % RM], adj_sb[:, t % RA], -1.0, BIG, ALU.add, ALU.mult) \
                    .then_inc(mask_ready, 1)

            def split_high(r, n):
                pool.wait_ge(hT_ready, due(r, 2 * BATCHES, 2 * n + 2))
                own_turn(pool, r, pool_turn)
                b = n % 2
                nc.gpsimd.tensor_scalar(h_hi[:, b], hT[:], 1.0, 0.0, ALU.mult, ALU.add).then_inc(split_part, 1)
                nc.gpsimd.tensor_scalar(u_hi[:, b], hT[:], a_sb[:, 0:1], 0.0, ALU.mult, ALU.add).then_inc(split_part, 1)
                nc.gpsimd.tensor_scalar(uT[:], hT[:], a_sb[:, 0:1], 0.0, ALU.mult, ALU.add).then_inc(u_ready, 1)

            def split_low_h(r, n):
                pool.wait_ge(split_part, due(r, 2 * BATCHES, 2 * n + 1))
                nc.gpsimd.tensor_tensor(h_lo[:, n % 2], hT[:], h_hi[:, n % 2].bitcast(F32), ALU.subtract) \
                    .then_inc(split_ready, 1)

            def split_low_u(r, n):
                pool.wait_ge(split_part, due(r, 2 * BATCHES, 2 * n + 2))
                pool.wait_ge(u_ready, due(r, BATCHES, n + 1))
                nc.gpsimd.tensor_tensor(u_lo[:, n % 2], uT[:], u_hi[:, n % 2].bitcast(F32), ALU.subtract) \
                    .then_inc(split_ready, 1)

            def norm(r, g):
                b = g % 2
                pool.wait_ge(moments_ready, due(r, GROUPS, g + 1))
                pool.wait_ge(normed_ready, due(r, GROUPS, START + g))
                own_turn(pool, r, pool_turn)
                nc.gpsimd.tensor_scalar(negmean[:], moments[:, b, :, 0], -1.0, 0.0, ALU.mult, ALU.add).then_inc(norm_step, 1)
                nc.gpsimd.tensor_scalar(rstd[:], moments[:, b, :, 1], EPS, 1.0, ALU.add, ALU.mult).then_inc(norm_step, 1)
                pool.wait_ge(norm_step, due(r, 3 * GROUPS, 3 * g + 2))
                nc.gpsimd.tensor_tensor(rstd[:], rstd[:], minus_half[:], ALU.pow).then_inc(norm_step, 1)
                pool.wait_ge(norm_step, due(r, 3 * GROUPS, 3 * g + 3))
                pool.wait_ge(normed_free, due(r, GROUPS, START + g - 1))
                own_turn(pool, r, pool_turn)
                for k in range(G):
                    ins = nc.gpsimd.tensor_scalar(normed[:, b, k], y[:, b, k], negmean[:, k:k + 1],
                                                  rstd[:, k:k + 1], ALU.add, ALU.mult)
                ins.then_inc(normed_ready, 1)

            pool.wait_ge(a_loaded, 64)
            split_high(0, 0)
            split_low_h(0, 0)
            split_low_u(0, 0)
            make_mask(0, 0)
            make_mask(0, 1)

            def step(r, s):
                n = s // TB + 1
                if s + 2 < T:
                    make_mask(r, s + 2)
                if n < B and s % TB == 3:
                    split_high(r, n)
                if n < B and s % TB == 4:
                    split_low_h(r, n)
                if n < B and s % TB == 5:
                    split_low_u(r, n)
                if (s - BACK) % G == 0 and s >= BACK:
                    norm(r, (s - BACK) // G)

            pool.sem_inc(normed_ready, START)
            steps(pool, step)

            def tile(n):
                pool.wait_ge(g_moments_ready, n + 1)
                pool.wait_ge(g_done, n + 1)
                pool.sem_inc(g_turn["pool"], 1)
                nc.gpsimd.tensor_scalar(negmean[:, 0:1], moments[:, 0, 0, 0:1], -1.0, 0.0, ALU.mult, ALU.add) \
                    .then_inc(g_norm_step, 1)
                nc.gpsimd.tensor_scalar(rstd[:, 0:1], moments[:, 0, 0, 1:2], EPS, 1.0, ALU.add, ALU.mult) \
                    .then_inc(g_norm_step, 1)
                pool.wait_ge(g_norm_step, n * 3 + 2)
                nc.gpsimd.tensor_tensor(rstd[:, 0:1], rstd[:, 0:1], minus_half[:, 0:1], ALU.pow) \
                    .then_inc(g_norm_step, 1)
                pool.wait_ge(g_norm_step, n * 3 + 3)
                pool.sem_inc(g_turn["pool"], 1)
                nc.gpsimd.tensor_scalar(normed[:, 0, 0], y[:, 0, 0], negmean[:, 0:1], rstd[:, 0:1],
                                        ALU.add, ALU.mult).then_inc(g_normed_ready, 1)

            general(pool, None, tile)

        @block.tensor
        def _(pe):
            def turn_x(r, n, half):
                if half == 0:
                    pe.wait_ge(x_turn_loaded, due(r, 16 * BATCHES, 16 * (n + 1)))
                    if n >= 2:
                        pe.wait_ge(y_ready, due(r, GROUPS, START + 2 * n - 4))
                else:
                    pe.wait_ge(hT_ready, due(r, 2 * BATCHES, 2 * n + 1))
                for k in range(G):
                    mm = nc.tensor.transpose(aux[:, k * P:(k + 1) * P], x_turn[:, half * G + k, :], ident[:])
                mm.then_inc(xT_ready, 1)

            def scores(r, t):
                J, b, slot = t % TB, t // TB % 2, t % 2
                if J == 0:
                    pe.wait_ge(split_ready, due(r, 2 * BATCHES, 2 * (t // TB) + 2))
                if t >= 2:
                    pe.wait_ge(leaky_ready, due(r, PERIOD, t - 1))
                    if (t - 2) % TB:
                        pe.wait_ge(old_masked, due(r, OLD * BATCHES, OLD * ((t - 2) // TB) + (t - 2) % TB))
                pieces = [(max(J * P, c), c + HALF) for c in (0, HALF) if J * P < c + HALF]
                rows = slice(J * P, (J + 1) * P)
                for n, (u, h) in enumerate([(u_lo, h_hi), (u_hi, h_lo), (u_hi, h_hi)]):
                    for c0, c1 in pieces:
                        mm = nc.tensor.matmul(S[:, slot, c0:c1], u[:, b, rows], h[:, b, c0:c1],
                                              start=(n == 0), stop=(n == 2))
                for K in range(J):
                    if K == J - 1:
                        pe.wait_ge(leaky_ready, due(r, PERIOD, t))
                    mm = nc.tensor.transpose(S[:, slot, K * P:(K + 1) * P],
                                             leaky_cols(K, J * P, (J + 1) * P), ident[:])
                mm.then_inc(S_ready, 1)

            def turn(r, t):
                pe.wait_ge(probs_ready, due(r, PERIOD, t + 1))
                for half in range(2):
                    if t >= 1:
                        pe.wait_ge(probsT_ready, due(r, 2 * PERIOD, 2 * t - 1 + half))
                    for k in range(G):
                        j = half * G + k
                        mm = nc.tensor.transpose(turned[:, half, k * P:(k + 1) * P],
                                                 probs[:, t % 2, j * P:(j + 1) * P], ident[:])
                    mm.then_inc(turned_ready, 1)

            def mix_part(r, g, q):
                b = g // 2 % 2
                if q == 0:
                    pe.wait_ge(probsT_ready, due(r, 2 * PERIOD, 2 * G * (g + 1)))
                    pe.wait_ge(x_loaded[b], due(r, 16, 16 * (g // 4 + 1)))
                    pe.wait_ge(mixT_ready, due(r, GROUPS, START + g))
                for j in (2 * q, 2 * q + 1):
                    mm = nc.tensor.matmul(mix[:], x_sb[:, b, j, :], probsT[:, g % 2, j, :],
                                          start=(j == 0), stop=(j == TB - 1))
                mm.then_inc(mix_step, 1)

            def back(r, g):
                pe.wait_ge(mixT_ready, due(r, GROUPS, START + g + 1))
                if g % 2 == 0 and g // 2 + 2 < B:
                    pe.wait_ge(hT_ready, due(r, 2 * BATCHES, 2 * (g // 2 + 3)))
                pe.wait_ge(y_ready, due(r, GROUPS, START + g))
                for k in range(G):
                    mm = nc.tensor.transpose(aux[:, k * P:(k + 1) * P], mixT[:, k * P:(k + 1) * P], ident[:])
                mm.then_inc(back_ready, 1)

            pe.wait_ge(consts_ready, 1)
            turn_x(0, 0, 0)
            turn_x(0, 0, 1)

            def step(r, s):
                n = s // TB + 1
                if s < T:
                    scores(r, s)
                if n < B and s % TB in (1, 2):
                    turn_x(r, n, s % TB - 1)
                if (s - BACK) % G == 0 and s >= BACK:
                    back(r, (s - BACK) // G)
                if 0 <= s - 2 < T:
                    turn(r, s - 2)
                g, q = divmod(s - MIX, G)
                if 0 <= g < NG:
                    mix_part(r, g, q)

            pe.sem_inc(back_ready, START)
            steps(pe, step)

            pe.wait_ge(odd_ready, 1)
            nc.tensor.matmul(aux[0:1, 0:1], odd_rows[:], ones[:], start=True, stop=True).then_inc(counted, 1)

            def turn_batch(b):
                pe.wait_ge(g_x_loaded, b * 16 + 16)
                for half in range(2):
                    if half:
                        pe.wait_ge(g_hT_ready, b * 2 + 1)
                    for k in range(G):
                        mm = nc.tensor.transpose(aux[:, k * P:(k + 1) * P], x_sb[:, 0, half * G + k], ident[:])
                    mm.then_inc(g_xT_ready, 1)
                pe.wait_ge(g_hT_ready, b * 2 + 2)
                pe.sem_inc(g_turn["pe"], 1)

            def tile(n):
                pe.wait_ge(g_loaded, n * 32 + 32)
                nc.tensor.transpose(turned[:, 0, 0:P], g_rows, ident[:]).then_inc(g_rowsT_ready, 1)
                pe.wait_ge(g_u_ready, n + 1)
                for k in range(R):
                    if k >= 2:
                        pe.wait_ge(g_cand_ready, n * R + k - 1)
                    for c in (0, HALF):
                        mm = nc.tensor.matmul(S[:, k % 2, c:c + HALF], g_u[:, k * P:(k + 1) * P], hT[:, c:c + HALF],
                                              start=True, stop=True)
                    mm.then_inc(g_S_ready, 1)
                pe.wait_ge(g_probs_ready, n + 1)
                for j in range(TB):
                    mm = nc.tensor.transpose(turned[:, j // G, j % G * P:(j % G + 1) * P],
                                             probs[:, 1, j * P:(j + 1) * P], ident[:])
                mm.then_inc(g_turned_ready, 1)
                pe.wait_ge(g_probsT_ready, n + 1)
                for j in range(TB):
                    mm = nc.tensor.matmul(mix[:, 0:D], g_probsT[:, j], x_sb[:, 0, j], start=(j == 0), stop=(j == TB - 1))
                mm.then_inc(g_mixed, 1)

            general(pe, turn_batch, tile)

        @block.scalar
        def _(act):
            act.wait_ge(consts_ready, 1)
            nc.scalar.activation(warm[:], ident[:, 0:1], ACT.Exp)

            def copy_x(r, n, half):
                act.wait_ge(xT_ready, due(r, 2 * BATCHES, 2 * n + 1 + half))
                if half == 0 and n >= 1:
                    act.wait_ge(split_ready, due(r, 2 * BATCHES, 2 * n))
                nc.scalar.copy(hT[:, half * HALF:(half + 1) * HALF], aux[:]).then_inc(hT_ready, 1)

            def copy_scores(r, t):
                J = t % TB
                act.wait_ge(S_ready, due(r, PERIOD, t + 1))
                nc.scalar.copy(leaky_cols(J, J * P, N), S[:, t % 2, J * P:N]).then_inc(copied, 1)

            def exp(r, t):
                act.wait_ge(masked_ready, due(r, PERIOD, t + 1))
                if t >= 2:
                    act.wait_ge(turned_ready, due(r, 2 * PERIOD, 2 * (t - 1)))
                c = t % PERIOD
                nc.scalar.activation(probs[:, t % 2], masked[:, t % 2], ACT.Exp, bias=negmax[:, c:c + 1],
                                     scale=-1.0, accum_out=rowsum[:, c:c + 1]).then_inc(probs_ready, 1)

            def copy_turned(r, t, half):
                g, k = t // G, t % G
                act.wait_ge(turned_ready, due(r, 2 * PERIOD, 2 * t + 1 + half))
                if g >= 2 and k == 0 and half == 0:
                    act.wait_ge(mix_step, due(r, PERIOD, G * (g - 1)))
                nc.scalar.copy(probsT[:, g % 2, half * G:(half + 1) * G, k * P:(k + 1) * P],
                               turned[:, half].rearrange("p (j i) -> p j i", j=G)).then_inc(probsT_ready, 1)

            def copy_mix(r, g):
                act.wait_ge(mix_step, due(r, PERIOD, G * (g + 1)))
                act.wait_ge(back_ready, due(r, GROUPS, START + g))
                nc.scalar.copy(mixT[:], mix[:]).then_inc(mixT_ready, 1)

            copy_x(0, 0, 0)
            copy_x(0, 0, 1)

            def step(r, s):
                n = s // TB + 1
                if (s - BACK + 1) % G == 0 and s >= BACK - 1:
                    copy_mix(r, (s - BACK + 1) // G)
                if s < T:
                    copy_scores(r, s)
                if 0 <= s - 1 < T:
                    exp(r, s - 1)
                if n < B and s % TB in (1, 2):
                    copy_x(r, n, s % TB - 1)
                if 0 <= s - 2 < T:
                    copy_turned(r, s - 2, 0)
                    copy_turned(r, s - 2, 1)

            act.sem_inc(mixT_ready, START)
            steps(act, step)

            def copy_batch(b):
                for half in range(2):
                    act.wait_ge(g_xT_ready, b * 2 + 1 + half)
                    nc.scalar.copy(hT[:, half * HALF:(half + 1) * HALF], aux[:]).then_inc(g_hT_ready, 1)

            def tile(n):
                act.wait_ge(g_max_ready, n + 1)
                nc.scalar.activation(probs[:, 1], g_best, ACT.Exp, bias=negmax[:, 0:1],
                                     accum_out=rowsum[:, 0:1]).then_inc(g_probs_ready, 1)
                act.wait_ge(g_turned_ready, n + 1)
                nc.scalar.copy(g_probsT, turned[:].rearrange("p h (j i) -> p (h j) i", j=G)).then_inc(g_probsT_ready, 1)

            general(act, copy_batch, tile)

        @block.vector
        def _(dve):
            def mask_scores(r, t):
                J, slot, c = t % TB, t % 2, t % PERIOD
                new, old = slice(J * P, N), slice(0, J * P)
                dve.wait_ge(copied, due(r, PERIOD, t + 1))
                kept = leaky_cols(J, J * P, N)
                nc.vector.scalar_tensor_tensor(out=kept, in0=S[:, slot, new], scalar=SLOPE, in1=kept,
                                               op0=ALU.mult, op1=ALU.max).then_inc(leaky_ready, 1)
                dve.wait_ge(mask_ready, due(r, PERIOD, t + 1))
                if t >= 2:
                    dve.wait_ge(probs_ready, due(r, PERIOD, t - 1))
                own_turn(dve, r, dve_turn)
                if J:
                    nc.vector.tensor_tensor_reduce(masked[:, slot, old], S[:, slot, old], mask[:, t % RM, old],
                                                   -1.0, 3e38, ALU.add, ALU.min, oldmin[:, slot:slot + 1]) \
                        .then_inc(old_masked, 1)
                    dve.wait_ge(old_masked, due(r, OLD * BATCHES, OLD * (t // TB) + J))
                dve.wait_ge(leaky_ready, due(r, PERIOD, t + 1))
                own_turn(dve, r, dve_turn)
                nc.vector.tensor_tensor_reduce(masked[:, slot, new], kept, mask[:, t % RM, new], -1.0,
                                               oldmin[:, slot:slot + 1] if J else 3e38,
                                               ALU.add, ALU.min, negmax[:, c:c + 1]).then_inc(masked_ready, 1)

            def residual(r, g):
                b, xb, c = g % 2, g // 2 % 2, g * G % PERIOD
                nc.vector.reciprocal(rinv[:], rowsum[:, c:c + G]).then_inc(rinv_ready, 1)
                dve.wait_ge(rinv_ready, due(r, GROUPS, g + 1))
                dve.wait_ge(back_ready, due(r, GROUPS, START + g + 1))
                dve.wait_ge(normed_ready, due(r, GROUPS, START + g - 1))
                for k in range(G):
                    ins = nc.vector.scalar_tensor_tensor(out=y[:, b, k], in0=aux[:, k * P:(k + 1) * P],
                                                         scalar=rinv[:, k:k + 1], in1=x_sb[:, xb, G * (g % 2) + k],
                                                         op0=ALU.mult, op1=ALU.add)
                ins.then_inc(y_ready, 1)
                dve.wait_ge(y_ready, due(r, GROUPS, START + g + 1))
                for k in range(G):
                    ins = nc.vector.bn_stats(stats[:, k], y[:, b, k])
                ins.then_inc(stats_ready, 1)
                dve.wait_ge(stats_ready, due(r, GROUPS, g + 1))
                own_turn(dve, r, dve_turn)
                for k in range(G):
                    ins = nc.vector.bn_aggr(moments[:, b, k], stats[:, k])
                ins.then_inc(moments_ready, 1)

            def check_batch(r, n):
                c = n * TB % PERIOD
                most, sums = negmax[:, c:c + TB], rowsum[:, c:c + TB]
                nc.vector.tensor_scalar(lifted[:], most, -BIG / 2, None, ALU.is_lt)
                nc.vector.tensor_scalar(uniform[:], sums, float(N), None, ALU.is_equal).then_inc(odd_step, 1)
                dve.wait_ge(odd_step, due(r, 4 * BATCHES, 4 * n + 1))
                nc.vector.scalar_tensor_tensor(out=uneven[:], in0=most, scalar=BIG / 2, in1=uniform[:],
                                               op0=ALU.is_gt, op1=ALU.is_gt).then_inc(odd_step, 1)
                dve.wait_ge(odd_step, due(r, 4 * BATCHES, 4 * n + 2))
                nc.vector.tensor_tensor(odd[:], odd[:], lifted[:], ALU.max).then_inc(odd_step, 1)
                dve.wait_ge(odd_step, due(r, 4 * BATCHES, 4 * n + 3))
                nc.vector.tensor_tensor(odd[:], odd[:], uneven[:], ALU.max).then_inc(odd_step, 1)

            def step(r, s):
                if s < T:
                    mask_scores(r, s)
                if (s - BACK) % G == 0 and s >= BACK:
                    residual(r, (s - BACK) // G)
                if s % TB == 2 and s > TB:
                    dve.wait_ge(probs_ready, due(r, PERIOD, s - 2))
                    check_batch(r, s // TB - 1)

            dve.sem_inc(y_ready, START)
            steps(dve, step)

            dve.wait_ge(odd_step, 4 * B)
            nc.vector.reduce_max(odd_rows[:], odd[:], AX.X).then_inc(odd_ready, 1)
            dve.wait_ge(counted, 1)
            nc.vector.tensor_copy(verdict[:], aux[0:1, 0:1]).then_inc(verdict_ready, 1)

            def tile(n):
                dve.wait_ge(g_rowsT_ready, n + 1)
                for k in range(R):
                    ins = nc.vector.tensor_scalar(g_u[:, k * P:(k + 1) * P], turned[:, 0, 0:P], a_sb[:, k:k + 1],
                                                  None, ALU.mult)
                ins.then_inc(g_u_ready, 1)
                for k in range(R):
                    if k:
                        dve.wait_ge(g_cand_ready, n * R + k)
                    nc.vector.tensor_scalar(mask[:, 0], adj_sb[:, 0], float(k + 1), -1.0, ALU.is_equal, ALU.add) \
                        .then_inc(g_edges_ready, 1)
                    dve.wait_ge(g_edges_ready, n * R + k + 1)
                    dve.wait_ge(g_S_ready, n * R + k + 1)
                    if k >= 2:
                        dve.wait_ge(g_best_ready, n * (R - 1) + k - 1)
                    nc.vector.scalar_tensor_tensor(out=masked[:, 0] if k else g_best, in0=mask[:, 0], scalar=BIG,
                                                   in1=S[:, k % 2], op0=ALU.mult, op1=ALU.add).then_inc(g_cand_ready, 1)
                    if k:
                        dve.wait_ge(g_cand_ready, n * R + k + 1)
                        nc.vector.tensor_tensor(g_best, g_best, masked[:, 0], ALU.max).then_inc(g_best_ready, 1)
                dve.wait_ge(g_best_ready, n * (R - 1) + R - 1)
                nc.vector.scalar_tensor_tensor(out=g_best, in0=g_best, scalar=SLOPE, in1=g_best,
                                               op0=ALU.mult, op1=ALU.max).then_inc(g_leaky_ready, 1)
                dve.wait_ge(g_leaky_ready, n + 1)
                nc.vector.tensor_reduce(negmax[:, 0:1], g_best, AX.X, ALU.max, negate=True).then_inc(g_max_ready, 1)
                dve.wait_ge(g_mixed, n + 1)
                nc.vector.reciprocal(rinv[:, 0:1], rowsum[:, 0:1]).then_inc(g_rinv_ready, 1)
                dve.wait_ge(g_rinv_ready, n + 1)
                nc.vector.scalar_tensor_tensor(out=y[:, 0, 0], in0=mix[:, 0:D], scalar=rinv[:, 0:1], in1=g_rows,
                                               op0=ALU.mult, op1=ALU.add).then_inc(g_y_ready, 1)
                dve.wait_ge(g_y_ready, n + 1)
                nc.vector.bn_stats(stats[:, 0], y[:, 0, 0]).then_inc(g_stats_ready, 1)
                dve.wait_ge(g_stats_ready, n + 1)
                dve.sem_inc(g_turn["dve"], 1)
                nc.vector.bn_aggr(moments[:, 0, 0], stats[:, 0]).then_inc(g_moments_ready, 1)

            general(dve, None, tile)


_INS=['x','adj','L0_gnn_a_0','L0_gnn_a_1','L0_gnn_a_2','L0_gnn_a_3']
def kernel(**inputs):
    import numpy as _np
    import concourse.bacc as _bacc
    from concourse import mybir as _mybir
    from concourse.bass_utils import run_bass_kernel_spmd as _run
    nc = _bacc.Bacc("TRN2", target_bir_lowering=False, num_devices=1)
    arrays, args = {}, []
    for name in _INS:
        a = _np.ascontiguousarray(inputs[name])
        arrays[f"in_{name}_dram"] = a
        args.append(nc.dram_tensor(f"in_{name}_dram", a.shape, _mybir.dt.from_np(a.dtype), kind="ExternalInput").ap())
    args.append(nc.dram_tensor("out_0_dram", (8,1024,128), _mybir.dt.float32, kind="ExternalOutput").ap())
    gat_residual_norm(nc, *args)
    r = _run(nc, [arrays], core_ids=[0])
    return r.results[0]["out_0_dram"]
```

```python
from contextlib import ExitStack

import concourse.bass as bass
from concourse import mybir

ALU = mybir.AluOpType
ACT = mybir.ActivationFunctionType
AX = mybir.AxisListType
F32 = mybir.dt.float32
F32R = mybir.dt.float32r
I32 = mybir.dt.int32

P = 128
SLOPE = 0.2
BIG = 2.0 ** 90
EPS = 1e-5
HALF = 512
PERIOD = 16


def gat_residual_norm(nc, x, adj, a_0, a_1, a_2, a_3, out):
    B, N, D = x.shape
    TB = N // P
    T = B * TB
    G = HALF // P
    NG = T // G
    BATCHES, GROUPS = PERIOD // TB, PERIOD // G
    assert D == P and N == 2 * HALF and T % PERIOD == 0 and PERIOD == 2 * TB
    FIRST = PERIOD
    LAST = T - PERIOD
    TURN, REST = 2, 11
    MIX, BACK, NORM, STORE = 6, 11, 15, 17
    END = G * (NG - 1) + STORE + 1
    OLD = TB - 1
    RA, RM = 8, 4

    with ExitStack() as ctx:
        def sb(name, shape, dt=F32):
            return ctx.enter_context(nc.sbuf_tensor(name, shape, dt))

        def psum(name, shape):
            return ctx.enter_context(nc.psum_tensor(name, shape, F32))

        def sem(name):
            return ctx.enter_context(nc.semaphore(name))

        adj_sb = sb("adj_sb", [P, RA, N], I32)
        mask = sb("mask", [P, RM, N])
        leaky = sb("leaky", [P, P * TB * (TB + 1) // 2])
        masked = sb("masked", [P, 2, N])
        probs = sb("probs", [P, 2, N])
        probsT = sb("probsT", [P, 2, TB, HALF])
        h_hi = sb("h_hi", [P, 2, N], F32R)
        h_lo = sb("h_lo", [P, 2, N], F32R)
        u_hi = sb("u_hi", [P, 2, N], F32R)
        u_lo = sb("u_lo", [P, 2, N], F32R)
        hT = sb("hT", [P, N])
        uT = sb("uT", [P, N])
        x_turn = sb("x_turn", [P, TB, D])
        x_sb = sb("x_sb", [P, 2, TB, D])
        mixT = sb("mixT", [P, HALF])
        y = sb("y", [P, 2, G, D])
        normed = sb("normed", [P, G, D])
        ident = sb("ident", [P, P])
        a_sb = sb("a_sb", [P, 4])
        minus_half = sb("minus_half", [P, G])
        negmax = sb("negmax", [P, PERIOD])
        oldmin = sb("oldmin", [P, 2])
        rowsum = sb("rowsum", [P, PERIOD])
        rinv = sb("rinv", [P, G])
        stats = sb("stats", [P, G, 6])
        moments = sb("moments", [P, 2, G, 2])
        rstd = sb("rstd", [P, G])
        negmean = sb("negmean", [P, G])
        lifted = sb("lifted", [P, TB])
        uniform = sb("uniform", [P, TB])
        uneven = sb("uneven", [P, TB])
        odd = sb("odd", [P, TB])
        warm = sb("warm", [P, 1])
        ones = sb("ones", [P, 1])
        odd_rows = sb("odd_rows", [P, 1])
        verdict = sb("verdict", [1, 1], I32)

        S = psum("S", [P, 2, N])
        turned = psum("turned", [P, 2, HALF])
        mix = psum("mix", [P, HALF])
        aux = psum("aux", [P, HALF])

        adj_loaded = [sem(f"adj_loaded{i}") for i in range(RA // 2)]
        a_loaded = sem("a_loaded")
        x_turn_loaded = sem("x_turn_loaded")
        x_loaded = [sem(f"x_loaded{i}") for i in range(2)]
        stored = sem("stored")
        consts_ready = sem("consts_ready")
        consts_step = sem("consts_step")
        mask_ready = sem("mask_ready")
        xT_ready = sem("xT_ready")
        hT_ready = sem("hT_ready")
        u_ready = sem("u_ready")
        split_part = sem("split_part")
        split_ready = sem("split_ready")
        S_ready = sem("S_ready")
        copied = sem("copied")
        leaky_ready = sem("leaky_ready")
        old_masked = sem("old_masked")
        masked_ready = sem("masked_ready")
        probs_ready = sem("probs_ready")
        turned_ready = sem("turned_ready")
        probsT_ready = sem("probsT_ready")
        mix_step = sem("mix_step")
        mixT_ready = sem("mixT_ready")
        back_ready = sem("back_ready")
        rinv_ready = sem("rinv_ready")
        y_ready = sem("y_ready")
        stats_ready = sem("stats_ready")
        moments_ready = sem("moments_ready")
        norm_step = sem("norm_step")
        normed_ready = sem("normed_ready")
        odd_step = sem("odd_step")
        odd_ready = sem("odd_ready")
        counted = sem("counted")
        verdict_ready = sem("verdict_ready")
        dve_turn = sem("dve_turn")
        pool_turn = sem("pool_turn")
        sp_turn = sem("sp_turn")

        g_loaded = sem("g_loaded")
        g_x_loaded = sem("g_x_loaded")
        g_xT_ready = sem("g_xT_ready")
        g_hT_ready = sem("g_hT_ready")
        g_rowsT_ready = sem("g_rowsT_ready")
        g_u_ready = sem("g_u_ready")
        g_S_ready = sem("g_S_ready")
        g_edges_ready = sem("g_edges_ready")
        g_cand_ready = sem("g_cand_ready")
        g_best_ready = sem("g_best_ready")
        g_leaky_ready = sem("g_leaky_ready")
        g_max_ready = sem("g_max_ready")
        g_probs_ready = sem("g_probs_ready")
        g_turned_ready = sem("g_turned_ready")
        g_probsT_ready = sem("g_probsT_ready")
        g_mixed = sem("g_mixed")
        g_rinv_ready = sem("g_rinv_ready")
        g_y_ready = sem("g_y_ready")
        g_stats_ready = sem("g_stats_ready")
        g_moments_ready = sem("g_moments_ready")
        g_norm_step = sem("g_norm_step")
        g_normed_ready = sem("g_normed_ready")
        g_stored = sem("g_stored")
        g_done = sem("g_done")
        g_turn = {e: sem(f"g_turn_{e}") for e in ("sp", "pool", "dve", "pe")}

        def due(r, per_period, count):
            return count if isinstance(r, int) else r * per_period + count

        def index(r, per_period, n):
            return n if isinstance(r, int) else r * per_period + n

        def steps(eng, step):
            for s in range(0, FIRST):
                step(0, s)
            with eng.Fori(0, (LAST - FIRST) // PERIOD) as r:
                for s in range(FIRST, FIRST + PERIOD):
                    step(r, s)
            for s in range(LAST, END):
                step(0, s)

        def own_turn(eng, r, turns):
            if not isinstance(r, int):
                eng.sem_inc(turns, 1)

        def leaky_cols(J, c0, c1):
            at = P * (TB * J - J * (J - 1) // 2) - P * J
            return leaky[:, at + c0:at + c1]

        out_g = out.rearrange("b (g k p) d -> (b g) p k d", k=G, p=P)
        adj_p = adj.rearrange("b (q k p) n -> (b q) p k n", k=2, p=P)
        x_b = x.rearrange("b (t p) d -> b p t d", p=P)

        R = 4
        g_rows, g_u, g_best = y[:, 1, 0], uT[:, 0:R * P], probs[:, 0]
        g_probsT = probsT[:, 0, :, 0:P]
        out_t = out.rearrange("b (t p) d -> (b t) p d", p=P)
        x_t = x.rearrange("b (t p) d -> (b t) p d", p=P)
        adj_t = adj.rearrange("b (t p) n -> (b t) p n", p=P)

        def general(eng, per_batch, per_tile):
            eng.wait_ge(verdict_ready, 1)
            rows = eng.value_load(verdict[0:1, 0:1])
            with eng.If(rows > 0):
                with eng.Fori(0, B) as b:
                    if per_batch:
                        per_batch(b)
                    with eng.Fori(0, TB) as t:
                        per_tile(b * TB + t)

        block = ctx.enter_context(nc.Block())

        @block.sync
        def _(sp):
            sp.dma_start(x_turn[:], x_b[0]).then_inc(x_turn_loaded, 16)
            sp.dma_start(adj_sb[:, 0:2, :], adj_p[0]).then_inc(adj_loaded[0], 16)
            for k, a in enumerate((a_0, a_1, a_2, a_3)):
                sp.dma_start(a_sb[:, k:k + 1], a).then_inc(a_loaded, 16)
            sp.dma_start(x_sb[:, 0], x_b[0]).then_inc(x_loaded[0], 16)
            sp.dma_start(adj_sb[:, 2:4, :], adj_p[1]).then_inc(adj_loaded[1], 16)
            sp.wait_ge(xT_ready, 2)
            sp.dma_start(x_turn[:], x_b[1]).then_inc(x_turn_loaded, 16)
            sp.dma_start(x_sb[:, 1], x_b[1]).then_inc(x_loaded[1], 16)
            for q in range(2, RA // 2):
                sp.dma_start(adj_sb[:, 2 * q:2 * q + 2, :], adj_p[q]).then_inc(adj_loaded[q], 16)

            def step(r, s):
                if s % 2 == 0 and s + RA < T:
                    sp.wait_ge(mask_ready, due(r, PERIOD, s + 2))
                    own_turn(sp, r, sp_turn)
                    q = (s + RA) // 2
                    sp.dma_start(adj_sb[:, s % RA:s % RA + 2, :], adj_p[index(r, PERIOD // 2, q)]) \
                        .then_inc(adj_loaded[q % (RA // 2)], 16)
                n = s // TB + 2
                if s % TB == TB - 3 and n < B:
                    sp.wait_ge(xT_ready, due(r, 2 * BATCHES, 2 * n))
                    own_turn(sp, r, sp_turn)
                    sp.dma_start(x_turn[:], x_b[index(r, BATCHES, n)]).then_inc(x_turn_loaded, 16)
                n = s // TB
                if s % TB == 3 and 2 <= n < B:
                    sp.wait_ge(y_ready, due(r, PERIOD, TB * (n - 1)))
                    own_turn(sp, r, sp_turn)
                    sp.dma_start(x_sb[:, n % 2], x_b[index(r, BATCHES, n)]).then_inc(x_loaded[n % 2], 16)
                g, at = divmod(s - STORE, G)
                if at == 0 and g >= 0:
                    sp.wait_ge(normed_ready, due(r, GROUPS, g + 1))
                    own_turn(sp, r, sp_turn)
                    sp.dma_start(out_g[index(r, GROUPS, g)], normed[:]).then_inc(stored, 16)

            steps(sp, step)
            sp.wait_ge(stored, 16 * NG)

            def load_x(b):
                sp.wait_ge(g_done, b * TB + 1)
                sp.sem_inc(g_turn["sp"], 1)
                sp.dma_start(x_sb[:, 0], x_b[b]).then_inc(g_x_loaded, 16)

            def tile(n):
                sp.wait_ge(g_done, n + 1)
                sp.sem_inc(g_turn["sp"], 1)
                sp.dma_start(adj_sb[:, 0], adj_t[n]).then_inc(g_loaded, 16)
                sp.dma_start(g_rows, x_t[n]).then_inc(g_loaded, 16)
                sp.wait_ge(g_normed_ready, n + 1)
                sp.sem_inc(g_turn["sp"], 1)
                sp.dma_start(out_t[n], normed[:, 0]).then_inc(g_stored, 16)
                sp.wait_ge(g_stored, n * 16 + 16)
                sp.sem_inc(g_done, 1)

            sp.sem_inc(g_done, 1)
            general(sp, load_x, tile)

        @block.gpsimd
        def _(pool):
            nc.gpsimd.memset(ident[:], 0.0).then_inc(consts_step, 1)
            nc.gpsimd.memset(minus_half[:], -0.5)
            nc.gpsimd.memset(ones[:], 1.0)
            nc.gpsimd.memset(odd[:], 0.0)
            pool.wait_ge(consts_step, 1)
            nc.gpsimd.affine_select(out=ident[:], in_=ident[:], compare_op=ALU.not_equal, fill=1.0, base=0,
                                    pattern=[[-1, P]], channel_multiplier=1).then_inc(consts_ready, 1)

            def make_mask(r, t):
                pool.wait_ge(adj_loaded[t // 2 % (RA // 2)], due(r, 16 * PERIOD // RA, 16 * (t // RA + 1)))
                if t >= RM:
                    pool.wait_ge(masked_ready, due(r, PERIOD, t - RM + 1))
                own_turn(pool, r, pool_turn)
                nc.gpsimd.tensor_scalar(mask[:, t % RM], adj_sb[:, t % RA], -1.0, BIG, ALU.add, ALU.mult) \
                    .then_inc(mask_ready, 1)

            def split_high(r, n):
                pool.wait_ge(hT_ready, due(r, 2 * BATCHES, 2 * n + 2))
                own_turn(pool, r, pool_turn)
                b = n % 2
                nc.gpsimd.tensor_scalar(h_hi[:, b], hT[:], 1.0, 0.0, ALU.mult, ALU.add).then_inc(split_part, 1)
                nc.gpsimd.tensor_scalar(u_hi[:, b], hT[:], a_sb[:, 0:1], 0.0, ALU.mult, ALU.add).then_inc(split_part, 1)
                nc.gpsimd.tensor_scalar(uT[:], hT[:], a_sb[:, 0:1], 0.0, ALU.mult, ALU.add).then_inc(u_ready, 1)

            def split_low_h(r, n):
                pool.wait_ge(split_part, due(r, 2 * BATCHES, 2 * n + 1))
                nc.gpsimd.tensor_tensor(h_lo[:, n % 2], hT[:], h_hi[:, n % 2].bitcast(F32), ALU.subtract) \
                    .then_inc(split_ready, 1)

            def split_low_u(r, n):
                pool.wait_ge(split_part, due(r, 2 * BATCHES, 2 * n + 2))
                pool.wait_ge(u_ready, due(r, BATCHES, n + 1))
                nc.gpsimd.tensor_tensor(u_lo[:, n % 2], uT[:], u_hi[:, n % 2].bitcast(F32), ALU.subtract) \
                    .then_inc(split_ready, 1)

            def norm(r, g):
                b = g % 2
                pool.wait_ge(moments_ready, due(r, PERIOD, G * (g + 1)))
                if g >= 1:
                    pool.wait_ge(normed_ready, due(r, GROUPS, g))
                own_turn(pool, r, pool_turn)
                nc.gpsimd.tensor_scalar(negmean[:], moments[:, b, :, 0], -1.0, 0.0, ALU.mult, ALU.add).then_inc(norm_step, 1)
                nc.gpsimd.tensor_scalar(rstd[:], moments[:, b, :, 1], EPS, 1.0, ALU.add, ALU.mult).then_inc(norm_step, 1)
                pool.wait_ge(norm_step, due(r, 3 * GROUPS, 3 * g + 2))
                nc.gpsimd.tensor_tensor(rstd[:], rstd[:], minus_half[:], ALU.pow).then_inc(norm_step, 1)
                pool.wait_ge(norm_step, due(r, 3 * GROUPS, 3 * g + 3))
                if g >= 1:
                    pool.wait_ge(stored, due(r, 16 * GROUPS, 16 * g))
                own_turn(pool, r, pool_turn)
                for k in range(G):
                    ins = nc.gpsimd.tensor_scalar(normed[:, k], y[:, b, k], negmean[:, k:k + 1],
                                                  rstd[:, k:k + 1], ALU.add, ALU.mult)
                ins.then_inc(normed_ready, 1)

            pool.wait_ge(a_loaded, 64)
            pool.wait_ge(hT_ready, 2)
            nc.gpsimd.tensor_scalar(u_hi[:, 0], hT[:], a_sb[:, 0:1], 0.0, ALU.mult, ALU.add).then_inc(split_part, 1)
            nc.gpsimd.tensor_scalar(uT[:], hT[:], a_sb[:, 0:1], 0.0, ALU.mult, ALU.add).then_inc(u_ready, 1)
            make_mask(0, 0)
            make_mask(0, 1)

            def step(r, s):
                n = s // TB + 1
                if s + 2 < T:
                    make_mask(r, s + 2)
                if n < B and s % TB == 3:
                    split_high(r, n)
                if n < B and s % TB == 4:
                    split_low_h(r, n)
                if n < B and s % TB == 5:
                    split_low_u(r, n)
                if (s - NORM) % G == 0 and s >= NORM:
                    norm(r, (s - NORM) // G)

            steps(pool, step)

            def tile(n):
                pool.wait_ge(g_moments_ready, n + 1)
                pool.wait_ge(g_done, n + 1)
                pool.sem_inc(g_turn["pool"], 1)
                nc.gpsimd.tensor_scalar(negmean[:, 0:1], moments[:, 0, 0, 0:1], -1.0, 0.0, ALU.mult, ALU.add) \
                    .then_inc(g_norm_step, 1)
                nc.gpsimd.tensor_scalar(rstd[:, 0:1], moments[:, 0, 0, 1:2], EPS, 1.0, ALU.add, ALU.mult) \
                    .then_inc(g_norm_step, 1)
                pool.wait_ge(g_norm_step, n * 3 + 2)
                nc.gpsimd.tensor_tensor(rstd[:, 0:1], rstd[:, 0:1], minus_half[:, 0:1], ALU.pow) \
                    .then_inc(g_norm_step, 1)
                pool.wait_ge(g_norm_step, n * 3 + 3)
                pool.sem_inc(g_turn["pool"], 1)
                nc.gpsimd.tensor_scalar(normed[:, 0], y[:, 0, 0], negmean[:, 0:1], rstd[:, 0:1],
                                        ALU.add, ALU.mult).then_inc(g_normed_ready, 1)

            general(pool, None, tile)

        @block.tensor
        def _(pe):
            def turn_x(r, n, half):
                if half == 0:
                    pe.wait_ge(x_turn_loaded, due(r, 16 * BATCHES, 16 * (n + 1)))
                if n >= 1:
                    pe.wait_ge(probsT_ready, due(r, 2 * PERIOD, 2 * (TB * (n - 1) + half)))
                elif half == 1:
                    pe.wait_ge(hT_ready, 1)
                for k in range(G):
                    mm = nc.tensor.transpose(turned[:, 0, k * P:(k + 1) * P], x_turn[:, half * G + k, :], ident[:])
                mm.then_inc(xT_ready, 1)

            def scores(r, t):
                J, b, slot = t % TB, t // TB % 2, t % 2
                if J == 0:
                    pe.wait_ge(split_ready, due(r, 2 * BATCHES, 2 * (t // TB) + 2))
                if t >= 2:
                    pe.wait_ge(leaky_ready, due(r, PERIOD, t - 1))
                    if (t - 2) % TB:
                        pe.wait_ge(old_masked, due(r, OLD * BATCHES, OLD * ((t - 2) // TB) + (t - 2) % TB))
                pieces = [(max(J * P, c), c + HALF) for c in (0, HALF) if J * P < c + HALF]
                rows = slice(J * P, (J + 1) * P)
                for n, (u, h) in enumerate([(u_lo, h_hi), (u_hi, h_lo), (u_hi, h_hi)]):
                    for c0, c1 in pieces:
                        mm = nc.tensor.matmul(S[:, slot, c0:c1], u[:, b, rows], h[:, b, c0:c1],
                                              start=(n == 0), stop=(n == 2))
                for K in range(J):
                    if K == J - 1:
                        pe.wait_ge(leaky_ready, due(r, PERIOD, t))
                    mm = nc.tensor.transpose(S[:, slot, K * P:(K + 1) * P],
                                             leaky_cols(K, J * P, (J + 1) * P), ident[:])
                mm.then_inc(S_ready, 1)

            def turn(r, t):
                pe.wait_ge(probs_ready, due(r, PERIOD, t + 1))
                n = (t + TURN - 1) // TB + 1
                if (t + TURN - 1) % TB in (1, 2) and n < B:
                    pe.wait_ge(hT_ready, due(r, 2 * BATCHES, 2 * n + (t + TURN - 1) % TB))
                for half in range(2):
                    if t >= 1:
                        pe.wait_ge(probsT_ready, due(r, 2 * PERIOD, 2 * t - 1 + half))
                    for k in range(G):
                        j = half * G + k
                        mm = nc.tensor.transpose(turned[:, half, k * P:(k + 1) * P],
                                                 probs[:, t % 2, j * P:(j + 1) * P], ident[:])
                    mm.then_inc(turned_ready, 1)

            def mix_part(r, g, q):
                b = g // 2 % 2
                if q == 0:
                    pe.wait_ge(probsT_ready, due(r, 2 * PERIOD, 2 * G * (g + 1)))
                    pe.wait_ge(x_loaded[b], due(r, 16, 16 * (g // 4 + 1)))
                    if g >= 1:
                        pe.wait_ge(mixT_ready, due(r, GROUPS, g))
                for j in (2 * q, 2 * q + 1):
                    mm = nc.tensor.matmul(mix[:], x_sb[:, b, j, :], probsT[:, g % 2, j, :],
                                          start=(j == 0), stop=(j == TB - 1))
                mm.then_inc(mix_step, 1)

            def back(r, g):
                pe.wait_ge(mixT_ready, due(r, GROUPS, g + 1))
                if g >= 1:
                    pe.wait_ge(y_ready, due(r, PERIOD, G * g))
                for k in range(G):
                    mm = nc.tensor.transpose(aux[:, k * P:(k + 1) * P], mixT[:, k * P:(k + 1) * P], ident[:])
                mm.then_inc(back_ready, 1)

            pe.wait_ge(consts_ready, 1)
            turn_x(0, 0, 0)
            turn_x(0, 0, 1)

            def step(r, s):
                n = s // TB + 1
                if s < T:
                    scores(r, s)
                g, at = divmod(s - BACK, G)
                if at == 0 and 0 <= g < NG:
                    back(r, g)
                if 0 <= s - TURN < T:
                    turn(r, s - TURN)
                g, q = divmod(s - MIX, G)
                if 0 <= g < NG:
                    mix_part(r, g, q)
                if n < B and s % TB in (1, 2):
                    turn_x(r, n, s % TB - 1)

            steps(pe, step)

            pe.wait_ge(odd_ready, 1)
            nc.tensor.matmul(aux[0:1, 0:1], odd_rows[:], ones[:], start=True, stop=True).then_inc(counted, 1)

            def turn_batch(b):
                pe.wait_ge(g_x_loaded, b * 16 + 16)
                for half in range(2):
                    if half:
                        pe.wait_ge(g_hT_ready, b * 2 + 1)
                    for k in range(G):
                        mm = nc.tensor.transpose(aux[:, k * P:(k + 1) * P], x_sb[:, 0, half * G + k], ident[:])
                    mm.then_inc(g_xT_ready, 1)
                pe.wait_ge(g_hT_ready, b * 2 + 2)
                pe.sem_inc(g_turn["pe"], 1)

            def tile(n):
                pe.wait_ge(g_loaded, n * 32 + 32)
                nc.tensor.transpose(turned[:, 0, 0:P], g_rows, ident[:]).then_inc(g_rowsT_ready, 1)
                pe.wait_ge(g_u_ready, n + 1)
                for k in range(R):
                    if k >= 2:
                        pe.wait_ge(g_cand_ready, n * R + k - 1)
                    for c in (0, HALF):
                        mm = nc.tensor.matmul(S[:, k % 2, c:c + HALF], g_u[:, k * P:(k + 1) * P], hT[:, c:c + HALF],
                                              start=True, stop=True)
                    mm.then_inc(g_S_ready, 1)
                pe.wait_ge(g_probs_ready, n + 1)
                for j in range(TB):
                    mm = nc.tensor.transpose(turned[:, j // G, j % G * P:(j % G + 1) * P],
                                             probs[:, 1, j * P:(j + 1) * P], ident[:])
                mm.then_inc(g_turned_ready, 1)
                pe.wait_ge(g_probsT_ready, n + 1)
                for j in range(TB):
                    mm = nc.tensor.matmul(mix[:, 0:D], g_probsT[:, j], x_sb[:, 0, j], start=(j == 0), stop=(j == TB - 1))
                mm.then_inc(g_mixed, 1)

            general(pe, turn_batch, tile)

        @block.scalar
        def _(act):
            act.wait_ge(consts_ready, 1)
            nc.scalar.activation(warm[:], ident[:, 0:1], ACT.Exp)

            def copy_x(r, n, half):
                act.wait_ge(xT_ready, due(r, 2 * BATCHES, 2 * n + 1 + half))
                if half == 0 and n >= 1:
                    act.wait_ge(split_ready, due(r, 2 * BATCHES, 2 * n))
                nc.scalar.copy(hT[:, half * HALF:(half + 1) * HALF], turned[:, 0]).then_inc(hT_ready, 1)

            def copy_scores(r, t):
                J = t % TB
                act.wait_ge(S_ready, due(r, PERIOD, t + 1))
                nc.scalar.copy(leaky_cols(J, J * P, N), S[:, t % 2, J * P:N]).then_inc(copied, 1)

            def exp(r, t):
                act.wait_ge(masked_ready, due(r, PERIOD, t + 1))
                if t >= 2:
                    act.wait_ge(turned_ready, due(r, 2 * PERIOD, 2 * (t - 1)))
                c = t % PERIOD
                nc.scalar.activation(probs[:, t % 2], masked[:, t % 2], ACT.Exp, bias=negmax[:, c:c + 1],
                                     scale=-1.0, accum_out=rowsum[:, c:c + 1]).then_inc(probs_ready, 1)

            def copy_turned(r, t, half):
                g, k = t // G, t % G
                act.wait_ge(turned_ready, due(r, 2 * PERIOD, 2 * t + 1 + half))
                if g >= 2 and k == 0 and half == 0:
                    act.wait_ge(mix_step, due(r, PERIOD, G * (g - 1)))
                nc.scalar.copy(probsT[:, g % 2, half * G:(half + 1) * G, k * P:(k + 1) * P],
                               turned[:, half].rearrange("p (j i) -> p j i", j=G)).then_inc(probsT_ready, 1)

            def copy_mix(r, g):
                act.wait_ge(mix_step, due(r, PERIOD, G * (g + 1)))
                if g >= 1:
                    act.wait_ge(back_ready, due(r, GROUPS, g))
                nc.scalar.copy(mixT[:], mix[:]).then_inc(mixT_ready, 1)

            copy_x(0, 0, 0)
            copy_x(0, 0, 1)

            def step(r, s):
                n = s // TB + 1
                g, at = divmod(s - MIX - G, G)
                if at == 0 and 0 <= g < NG:
                    copy_mix(r, g)
                if s < T:
                    copy_scores(r, s)
                if 0 <= s - 1 < T:
                    exp(r, s - 1)
                if 0 <= s - TURN < T:
                    copy_turned(r, s - TURN, 0)
                    copy_turned(r, s - TURN, 1)
                if n < B and s % TB in (1, 2):
                    copy_x(r, n, s % TB - 1)

            steps(act, step)

            def copy_batch(b):
                for half in range(2):
                    act.wait_ge(g_xT_ready, b * 2 + 1 + half)
                    nc.scalar.copy(hT[:, half * HALF:(half + 1) * HALF], aux[:]).then_inc(g_hT_ready, 1)

            def tile(n):
                act.wait_ge(g_max_ready, n + 1)
                nc.scalar.activation(probs[:, 1], g_best, ACT.Exp, bias=negmax[:, 0:1],
                                     accum_out=rowsum[:, 0:1]).then_inc(g_probs_ready, 1)
                act.wait_ge(g_turned_ready, n + 1)
                nc.scalar.copy(g_probsT, turned[:].rearrange("p h (j i) -> p (h j) i", j=G)).then_inc(g_probsT_ready, 1)

            general(act, copy_batch, tile)

        @block.vector
        def _(dve):
            def leak(r, t):
                J = t % TB
                kept = leaky_cols(J, J * P, N)
                dve.wait_ge(copied, due(r, PERIOD, t + 1))
                nc.vector.scalar_tensor_tensor(out=kept, in0=S[:, t % 2, J * P:N], scalar=SLOPE, in1=kept,
                                               op0=ALU.mult, op1=ALU.max).then_inc(leaky_ready, 1)

            def mask_old(r, t):
                J, slot = t % TB, t % 2
                dve.wait_ge(mask_ready, due(r, PERIOD, t + 1))
                if t >= 2:
                    dve.wait_ge(probs_ready, due(r, PERIOD, t - 1))
                own_turn(dve, r, dve_turn)
                if J:
                    old = slice(0, J * P)
                    nc.vector.tensor_tensor_reduce(masked[:, slot, old], S[:, slot, old], mask[:, t % RM, old],
                                                   -1.0, 3e38, ALU.add, ALU.min, oldmin[:, slot:slot + 1]) \
                        .then_inc(old_masked, 1)

            def mask_new(r, t):
                J, slot, c = t % TB, t % 2, t % PERIOD
                new = slice(J * P, N)
                dve.wait_ge(leaky_ready, due(r, PERIOD, t + 1))
                if J:
                    dve.wait_ge(old_masked, due(r, OLD * BATCHES, OLD * (t // TB) + J))
                own_turn(dve, r, dve_turn)
                nc.vector.tensor_tensor_reduce(masked[:, slot, new], leaky_cols(J, J * P, N), mask[:, t % RM, new],
                                               -1.0, oldmin[:, slot:slot + 1] if J else 3e38,
                                               ALU.add, ALU.min, negmax[:, c:c + 1]).then_inc(masked_ready, 1)

            def invert(r, g):
                c = g * G % PERIOD
                if g >= 1:
                    dve.wait_ge(y_ready, due(r, PERIOD, G * g))
                dve.wait_ge(probs_ready, due(r, PERIOD, G * (g + 1)))
                nc.vector.reciprocal(rinv[:], rowsum[:, c:c + G]).then_inc(rinv_ready, 1)

            def residual(r, t):
                g, k = divmod(t, G)
                if k == 0:
                    dve.wait_ge(rinv_ready, due(r, GROUPS, g + 1))
                    dve.wait_ge(back_ready, due(r, GROUPS, g + 1))
                    if g >= 2:
                        dve.wait_ge(normed_ready, due(r, GROUPS, g - 1))
                nc.vector.scalar_tensor_tensor(out=y[:, g % 2, k], in0=aux[:, k * P:(k + 1) * P],
                                               scalar=rinv[:, k:k + 1], in1=x_sb[:, t // TB % 2, t % TB],
                                               op0=ALU.mult, op1=ALU.add).then_inc(y_ready, 1)

            def gather_stats(r, t):
                g, k = divmod(t, G)
                dve.wait_ge(y_ready, due(r, PERIOD, t + 1))
                nc.vector.bn_stats(stats[:, k], y[:, g % 2, k]).then_inc(stats_ready, 1)

            def find_moments(r, t):
                g, k = divmod(t, G)
                dve.wait_ge(stats_ready, due(r, PERIOD, t + 1))
                own_turn(dve, r, dve_turn)
                nc.vector.bn_aggr(moments[:, g % 2, k], stats[:, k]).then_inc(moments_ready, 1)

            def check_batch(r, n):
                c = n * TB % PERIOD
                most, sums = negmax[:, c:c + TB], rowsum[:, c:c + TB]
                nc.vector.tensor_scalar(lifted[:], most, -BIG / 2, None, ALU.is_lt)
                nc.vector.tensor_scalar(uniform[:], sums, float(N), None, ALU.is_equal).then_inc(odd_step, 1)
                dve.wait_ge(odd_step, due(r, 4 * BATCHES, 4 * n + 1))
                nc.vector.scalar_tensor_tensor(out=uneven[:], in0=most, scalar=BIG / 2, in1=uniform[:],
                                               op0=ALU.is_gt, op1=ALU.is_gt).then_inc(odd_step, 1)
                dve.wait_ge(odd_step, due(r, 4 * BATCHES, 4 * n + 2))
                nc.vector.tensor_tensor(odd[:], odd[:], lifted[:], ALU.max).then_inc(odd_step, 1)
                dve.wait_ge(odd_step, due(r, 4 * BATCHES, 4 * n + 3))
                nc.vector.tensor_tensor(odd[:], odd[:], uneven[:], ALU.max).then_inc(odd_step, 1)

            dve.wait_ge(hT_ready, 2)
            nc.vector.tensor_copy(h_hi[:, 0], hT[:]).then_inc(split_part, 1)
            dve.wait_ge(u_ready, 1)
            dve.wait_ge(split_part, 2)
            nc.vector.tensor_tensor(h_lo[:, 0], hT[:], h_hi[:, 0].bitcast(F32), ALU.subtract).then_inc(split_ready, 1)
            nc.vector.tensor_tensor(u_lo[:, 0], uT[:], u_hi[:, 0].bitcast(F32), ALU.subtract).then_inc(split_ready, 1)

            def step(r, s):
                rest = s - REST if 0 <= s - REST < T else None
                if s < T:
                    leak(r, s)
                if rest is not None and rest % G == 0:
                    invert(r, rest // G)
                if s < T:
                    mask_old(r, s)
                if rest is not None:
                    residual(r, rest)
                if s < T:
                    mask_new(r, s)
                if rest is not None:
                    gather_stats(r, rest)
                if s % TB == 2 and TB < s < T + TB:
                    dve.wait_ge(probs_ready, due(r, PERIOD, s - 2))
                    check_batch(r, s // TB - 1)
                if rest is not None:
                    find_moments(r, rest)

            steps(dve, step)

            dve.wait_ge(odd_step, 4 * B)
            nc.vector.reduce_max(odd_rows[:], odd[:], AX.X).then_inc(odd_ready, 1)
            dve.wait_ge(counted, 1)
            nc.vector.tensor_copy(verdict[:], aux[0:1, 0:1]).then_inc(verdict_ready, 1)

            def tile(n):
                dve.wait_ge(g_rowsT_ready, n + 1)
                for k in range(R):
                    ins = nc.vector.tensor_scalar(g_u[:, k * P:(k + 1) * P], turned[:, 0, 0:P], a_sb[:, k:k + 1],
                                                  None, ALU.mult)
                ins.then_inc(g_u_ready, 1)
                for k in range(R):
                    if k:
                        dve.wait_ge(g_cand_ready, n * R + k)
                    nc.vector.tensor_scalar(mask[:, 0], adj_sb[:, 0], float(k + 1), -1.0, ALU.is_equal, ALU.add) \
                        .then_inc(g_edges_ready, 1)
                    dve.wait_ge(g_edges_ready, n * R + k + 1)
                    dve.wait_ge(g_S_ready, n * R + k + 1)
                    if k >= 2:
                        dve.wait_ge(g_best_ready, n * (R - 1) + k - 1)
                    nc.vector.scalar_tensor_tensor(out=masked[:, 0] if k else g_best, in0=mask[:, 0], scalar=BIG,
                                                   in1=S[:, k % 2], op0=ALU.mult, op1=ALU.add).then_inc(g_cand_ready, 1)
                    if k:
                        dve.wait_ge(g_cand_ready, n * R + k + 1)
                        nc.vector.tensor_tensor(g_best, g_best, masked[:, 0], ALU.max).then_inc(g_best_ready, 1)
                dve.wait_ge(g_best_ready, n * (R - 1) + R - 1)
                nc.vector.scalar_tensor_tensor(out=g_best, in0=g_best, scalar=SLOPE, in1=g_best,
                                               op0=ALU.mult, op1=ALU.max).then_inc(g_leaky_ready, 1)
                dve.wait_ge(g_leaky_ready, n + 1)
                nc.vector.tensor_reduce(negmax[:, 0:1], g_best, AX.X, ALU.max, negate=True).then_inc(g_max_ready, 1)
                dve.wait_ge(g_mixed, n + 1)
                nc.vector.reciprocal(rinv[:, 0:1], rowsum[:, 0:1]).then_inc(g_rinv_ready, 1)
                dve.wait_ge(g_rinv_ready, n + 1)
                nc.vector.scalar_tensor_tensor(out=y[:, 0, 0], in0=mix[:, 0:D], scalar=rinv[:, 0:1], in1=g_rows,
                                               op0=ALU.mult, op1=ALU.add).then_inc(g_y_ready, 1)
                dve.wait_ge(g_y_ready, n + 1)
                nc.vector.bn_stats(stats[:, 0], y[:, 0, 0]).then_inc(g_stats_ready, 1)
                dve.wait_ge(g_stats_ready, n + 1)
                dve.sem_inc(g_turn["dve"], 1)
                nc.vector.bn_aggr(moments[:, 0, 0], stats[:, 0]).then_inc(g_moments_ready, 1)

            general(dve, None, tile)


_INS=['x','adj','L0_gnn_a_0','L0_gnn_a_1','L0_gnn_a_2','L0_gnn_a_3']
def kernel(**inputs):
    import numpy as _np
    import concourse.bacc as _bacc
    from concourse import mybir as _mybir
    from concourse.bass_utils import run_bass_kernel_spmd as _run
    nc = _bacc.Bacc("TRN2", target_bir_lowering=False, num_devices=1)
    arrays, args = {}, []
    for name in _INS:
        a = _np.ascontiguousarray(inputs[name])
        arrays[f"in_{name}_dram"] = a
        args.append(nc.dram_tensor(f"in_{name}_dram", a.shape, _mybir.dt.from_np(a.dtype), kind="ExternalInput").ap())
    args.append(nc.dram_tensor("out_0_dram", (8,1024,128), _mybir.dt.float32, kind="ExternalOutput").ap())
    gat_residual_norm(nc, *args)
    r = _run(nc, [arrays], core_ids=[0])
    return r.results[0]["out_0_dram"]
```

```python
from contextlib import ExitStack

import concourse.bass as bass
from concourse import mybir

ALU = mybir.AluOpType
ACT = mybir.ActivationFunctionType
AX = mybir.AxisListType
F32 = mybir.dt.float32
F32R = mybir.dt.float32r
I32 = mybir.dt.int32

P = 128
SLOPE = 0.2
BIG = 2.0 ** 90
EPS = 1e-5
HALF = 512
PERIOD = 16


def gat_residual_norm(nc, x, adj, a_0, a_1, a_2, a_3, out):
    B, N, D = x.shape
    TB = N // P
    T = B * TB
    G = HALF // P
    NG = T // G
    BATCHES, GROUPS = PERIOD // TB, PERIOD // G
    assert D == P and N == 2 * HALF and T % PERIOD == 0 and PERIOD == 2 * TB
    FIRST = PERIOD
    LAST = T - PERIOD
    TURN, REST = 2, 11
    MIX, BACK, NORM, STORE = 6, 11, 15, 17
    END = G * (NG - 1) + STORE + 1
    LAST_G = NG - 1
    PAIR = 2 * P
    LATE = G - 1
    MIX_ORDER = (0, 1, 2, 4, 5, 6, 7, LATE)
    OLD = TB - 1
    RA = 8

    with ExitStack() as ctx:
        def sb(name, shape, dt=F32):
            return ctx.enter_context(nc.sbuf_tensor(name, shape, dt))

        def psum(name, shape):
            return ctx.enter_context(nc.psum_tensor(name, shape, F32))

        def sem(name):
            return ctx.enter_context(nc.semaphore(name))

        adj_sb = sb("adj_sb", [P, RA, N], I32)
        leaky = sb("leaky", [P, P * TB * (TB + 1) // 2])
        masked = sb("masked", [P, 2, N])
        probs = sb("probs", [P, 2, N])
        probsT = sb("probsT", [P, 2, G, HALF])
        probsT_hi = sb("probsT_hi", [P, 2, G, HALF], F32R)
        probsT_lo = sb("probsT_lo", [P, 2, G, HALF], F32R)
        late_hi = sb("late_hi", [P, HALF], F32R)
        late_lo = sb("late_lo", [P, HALF], F32R)
        x_hi = sb("x_hi", [P, 2, TB - LATE, D], F32R)
        x_lo = sb("x_lo", [P, 2, TB - LATE, D], F32R)
        h_hi = sb("h_hi", [P, 2, N], F32R)
        h_lo = sb("h_lo", [P, 2, N], F32R)
        u_hi = sb("u_hi", [P, 2, N], F32R)
        u_lo = sb("u_lo", [P, 2, N], F32R)
        hT = sb("hT", [P, N])
        u_sb = sb("u_sb", [P, N])
        x_turn = sb("x_turn", [P, TB, D])
        x_sb = sb("x_sb", [P, 2, TB, D])
        mixT = sb("mixT", [P, HALF])
        y = sb("y", [P, 2, G, D])
        normed = sb("normed", [P, 2, G, D])
        ident = sb("ident", [P, P])
        a_sb = sb("a_sb", [P, 4])
        minus_half = sb("minus_half", [P, G])
        negmax = sb("negmax", [P, PERIOD])
        oldmin = sb("oldmin", [P, 2])
        rowsum = sb("rowsum", [P, PERIOD])
        rinv = sb("rinv", [P, G])
        stats = sb("stats", [P, G, 6])
        moments = sb("moments", [P, 2, G, 2])
        rstd = sb("rstd", [P, 2, G])
        negmean = sb("negmean", [P, 2, G])
        lifted = sb("lifted", [P, TB])
        uniform = sb("uniform", [P, TB])
        uneven = sb("uneven", [P, TB])
        odd = sb("odd", [P, TB])
        warm = sb("warm", [P, 1])
        ones = sb("ones", [P, 1])
        odd_rows = sb("odd_rows", [P, 1])
        verdict = sb("verdict", [1, 1], I32)

        S = psum("S", [P, 2, N])
        turned = psum("turned", [P, 2, HALF])
        mix = psum("mix", [P, HALF])
        aux = psum("aux", [P, HALF])

        adj_loaded = [sem(f"adj_loaded{i}") for i in range(RA // 2)]
        a_loaded = sem("a_loaded")
        a_rest_loaded = sem("a_rest_loaded")
        x_first_loaded = [sem(f"x_first_loaded{i}") for i in range(2)]
        x_turn_loaded = sem("x_turn_loaded")
        x_loaded = [sem(f"x_loaded{i}") for i in range(2)]
        stored = sem("stored")
        last_stored = sem("last_stored")
        consts_ready = sem("consts_ready")
        consts_step = sem("consts_step")
        mask_ready = sem("mask_ready")
        xT_ready = sem("xT_ready")
        hT_ready = sem("hT_ready")
        h_hi_ready = sem("h_hi_ready")
        u_hi_ready = sem("u_hi_ready")
        h_lo_ready = sem("h_lo_ready")
        u_ready = sem("u_ready")
        u_lo_ready = sem("u_lo_ready")
        first_part = sem("first_part")
        first_u_hi_ready = sem("first_u_hi_ready")
        first_u_lo_ready = sem("first_u_lo_ready")
        x_hi_ready = sem("x_hi_ready")
        x_lo_ready = sem("x_lo_ready")
        S_ready = sem("S_ready")
        copied = sem("copied")
        leaky_ready = sem("leaky_ready")
        old_masked = sem("old_masked")
        masked_ready = sem("masked_ready")
        probs_ready = sem("probs_ready")
        turned_ready = sem("turned_ready")
        probsT_ready = sem("probsT_ready")
        probsT_hi_ready = sem("probsT_hi_ready")
        probsT_lo_ready = sem("probsT_lo_ready")
        mix_step = sem("mix_step")
        mixT_ready = sem("mixT_ready")
        back_ready = sem("back_ready")
        last_mixed = sem("last_mixed")
        last_mixT_ready = sem("last_mixT_ready")
        last_back_ready = sem("last_back_ready")
        late_hi_ready = sem("late_hi_ready")
        late_lo_ready = sem("late_lo_ready")
        rinv_ready = sem("rinv_ready")
        y_ready = sem("y_ready")
        stats_ready = sem("stats_ready")
        moments_ready = sem("moments_ready")
        norm_step = sem("norm_step")
        normed_ready = sem("normed_ready")
        odd_step = sem("odd_step")
        odd_ready = sem("odd_ready")
        counted = sem("counted")
        verdict_ready = sem("verdict_ready")
        dve_turn = sem("dve_turn")
        pool_turn = sem("pool_turn")
        sp_turn = sem("sp_turn")

        g_loaded = sem("g_loaded")
        g_x_loaded = sem("g_x_loaded")
        g_xT_ready = sem("g_xT_ready")
        g_hT_ready = sem("g_hT_ready")
        g_rowsT_ready = sem("g_rowsT_ready")
        g_u_ready = sem("g_u_ready")
        g_S_ready = sem("g_S_ready")
        g_edges_ready = sem("g_edges_ready")
        g_cand_ready = sem("g_cand_ready")
        g_best_ready = sem("g_best_ready")
        g_leaky_ready = sem("g_leaky_ready")
        g_max_ready = sem("g_max_ready")
        g_probs_ready = sem("g_probs_ready")
        g_turned_ready = sem("g_turned_ready")
        g_probsT_ready = sem("g_probsT_ready")
        g_mixed = sem("g_mixed")
        g_rinv_ready = sem("g_rinv_ready")
        g_y_ready = sem("g_y_ready")
        g_stats_ready = sem("g_stats_ready")
        g_moments_ready = sem("g_moments_ready")
        g_norm_step = sem("g_norm_step")
        g_normed_ready = sem("g_normed_ready")
        g_stored = sem("g_stored")
        g_done = sem("g_done")
        g_turn = {e: sem(f"g_turn_{e}") for e in ("sp", "pool", "dve", "pe")}

        def due(r, per_period, count):
            return count if isinstance(r, int) else r * per_period + count

        def index(r, per_period, n):
            return n if isinstance(r, int) else r * per_period + n

        def steps(eng, step):
            for s in range(0, FIRST):
                step(0, s)
            with eng.Fori(0, (LAST - FIRST) // PERIOD) as r:
                for s in range(FIRST, FIRST + PERIOD):
                    step(r, s)
            for s in range(LAST, END):
                step(0, s)

        def own_turn(eng, r, turns):
            if not isinstance(r, int):
                eng.sem_inc(turns, 1)

        def x_turned_in(s):
            if s == 0:
                return [(1, 0), (1, 1)]
            n, half = s // TB + 2, s % TB - (TB - 2)
            return [(n, half)] if half >= 0 and n < B else []

        def leaky_cols(J, c0, c1):
            at = P * (TB * J - J * (J - 1) // 2) - P * J
            return leaky[:, at + c0:at + c1]

        last_mixT = masked[:, 0]
        out_g = out.rearrange("b (g k p) d -> (b g) p k d", k=G, p=P)
        adj_p = adj.rearrange("b (q k p) n -> (b q) p k n", k=2, p=P)
        x_b = x.rearrange("b (t p) d -> b p t d", p=P)

        R = 4
        mask = adj_sb[:].bitcast(F32)
        g_rows, g_u, g_best, g_mask = y[:, 1, 0], x_turn, probs[:, 0], mask[:, 1]
        g_probsT = probsT[:, 0, 0:2].rearrange("p a (j i) -> p (a j) i", i=P)
        out_t = out.rearrange("b (t p) d -> (b t) p d", p=P)
        x_t = x.rearrange("b (t p) d -> (b t) p d", p=P)
        adj_t = adj.rearrange("b (t p) n -> (b t) p n", p=P)

        def general(eng, per_batch, per_tile):
            eng.wait_ge(verdict_ready, 1)
            rows = eng.value_load(verdict[0:1, 0:1])
            with eng.If(rows > 0):
                with eng.Fori(0, B) as b:
                    if per_batch:
                        per_batch(b)
                    with eng.Fori(0, TB) as t:
                        per_tile(b * TB + t)

        block = ctx.enter_context(nc.Block())

        @block.sync
        def _(sp):
            sp.dma_start(a_sb[:, 0:1], a_0).then_inc(a_loaded, 16)
            for half in range(2):
                sp.dma_start(x_turn[:, half * G:(half + 1) * G], x_b[0][:, half * G:(half + 1) * G]) \
                    .then_inc(x_first_loaded[half], 16)
            sp.dma_start(adj_sb[:, 0:2, :], adj_p[0]).then_inc(adj_loaded[0], 16)
            sp.wait_ge(xT_ready, 2)
            sp.dma_start(x_turn[:], x_b[1]).then_inc(x_turn_loaded, 16)
            for q in range(1, RA // 2):
                sp.dma_start(adj_sb[:, 2 * q:2 * q + 2, :], adj_p[q]).then_inc(adj_loaded[q], 16)
                if q < 3:
                    sp.dma_start(x_sb[:, q - 1], x_b[q - 1]).then_inc(x_loaded[q - 1], 16)
            for k, a in ((1, a_1), (2, a_2), (3, a_3)):
                sp.dma_start(a_sb[:, k:k + 1], a).then_inc(a_rest_loaded, 16)

            def step(r, s):
                n = s // TB
                if s % TB == 2 and 2 <= n < B:
                    sp.wait_ge(y_ready, due(r, PERIOD, TB * (n - 1)))
                    own_turn(sp, r, sp_turn)
                    sp.dma_start(x_sb[:, n % 2], x_b[index(r, BATCHES, n)]).then_inc(x_loaded[n % 2], 16)
                if s % 2 == 0 and s + RA < T:
                    sp.wait_ge(masked_ready, due(r, PERIOD, s + 2))
                    own_turn(sp, r, sp_turn)
                    q = (s + RA) // 2
                    sp.dma_start(adj_sb[:, s % RA:s % RA + 2, :], adj_p[index(r, PERIOD // 2, q)]) \
                        .then_inc(adj_loaded[q % (RA // 2)], 16)
                n = s // TB + 2
                if s % TB == 1 and n < B:
                    sp.wait_ge(xT_ready, due(r, 2 * BATCHES, 2 * n))
                    own_turn(sp, r, sp_turn)
                    sp.dma_start(x_turn[:], x_b[index(r, BATCHES, n)]).then_inc(x_turn_loaded, 16)
                g, at = divmod(s - STORE, G)
                if at == 0 and 0 <= g < LAST_G - 1:
                    sp.wait_ge(normed_ready, due(r, GROUPS, g + 1))
                    own_turn(sp, r, sp_turn)
                    sp.dma_start(out_g[index(r, GROUPS, g)], normed[:, 0]).then_inc(stored, 16)

            steps(sp, step)
            sp.wait_ge(normed_ready, LAST_G)
            sp.dma_start(out_g[LAST_G - 1], normed[:, 1]).then_inc(last_stored, 16)
            for pair in range(2):
                k = slice(2 * pair, 2 * pair + 2)
                sp.wait_ge(normed_ready, LAST_G + 1 + pair)
                sp.dma_start(out_g[LAST_G][:, k], normed[:, 0, k]).then_inc(last_stored, 16)
            sp.wait_ge(stored, 16 * (LAST_G - 1))
            sp.wait_ge(last_stored, 16 * 3)

            def load_x(b):
                sp.wait_ge(g_done, b * TB + 1)
                sp.sem_inc(g_turn["sp"], 1)
                sp.dma_start(x_sb[:, 0], x_b[b]).then_inc(g_x_loaded, 16)

            def tile(n):
                sp.wait_ge(g_done, n + 1)
                sp.sem_inc(g_turn["sp"], 1)
                sp.dma_start(adj_sb[:, 0], adj_t[n]).then_inc(g_loaded, 16)
                sp.dma_start(g_rows, x_t[n]).then_inc(g_loaded, 16)
                sp.wait_ge(g_normed_ready, n + 1)
                sp.sem_inc(g_turn["sp"], 1)
                sp.dma_start(out_t[n], normed[:, 0, 0]).then_inc(g_stored, 16)
                sp.wait_ge(g_stored, n * 16 + 16)
                sp.sem_inc(g_done, 1)

            sp.sem_inc(g_done, 1)
            general(sp, load_x, tile)

        @block.gpsimd
        def _(pool):
            nc.gpsimd.memset(ident[:], 0.0).then_inc(consts_step, 1)
            nc.gpsimd.memset(minus_half[:], -0.5)
            nc.gpsimd.memset(ones[:], 1.0)
            nc.gpsimd.memset(odd[:], 0.0)
            pool.wait_ge(consts_step, 1)
            nc.gpsimd.affine_select(out=ident[:], in_=ident[:], compare_op=ALU.not_equal, fill=1.0, base=0,
                                    pattern=[[-1, P]], channel_multiplier=1).then_inc(consts_ready, 1)

            def make_mask(r, t):
                pool.wait_ge(adj_loaded[t // 2 % (RA // 2)], due(r, 16 * PERIOD // RA, 16 * (t // RA + 1)))
                own_turn(pool, r, pool_turn)
                nc.gpsimd.tensor_scalar(mask[:, t % RA], adj_sb[:, t % RA], -1.0, BIG, ALU.add, ALU.mult) \
                    .then_inc(mask_ready, 1)

            def split_high_u(r, n):
                pool.wait_ge(hT_ready, due(r, 2 * BATCHES, 2 * n + 2))
                own_turn(pool, r, pool_turn)
                nc.gpsimd.tensor_scalar(u_hi[:, n % 2], hT[:], a_sb[:, 0:1], 0.0, ALU.mult, ALU.add) \
                    .then_inc(u_hi_ready, 1)

            def split_low_h(r, n):
                pool.wait_ge(h_hi_ready, due(r, BATCHES, n + 1))
                nc.gpsimd.tensor_tensor(h_lo[:, n % 2], hT[:], h_hi[:, n % 2].bitcast(F32), ALU.subtract) \
                    .then_inc(h_lo_ready, 1)

            def split_late(r, g):
                whole = probsT[:, g % 2, LATE]
                pool.wait_ge(probsT_ready, due(r, PERIOD, G * (g + 1)))
                if g >= 1:
                    pool.wait_ge(mix_step, due(r, PERIOD, G * g))
                own_turn(pool, r, pool_turn)
                nc.gpsimd.tensor_scalar(late_hi[:], whole, 1.0, 0.0, ALU.mult, ALU.add).then_inc(late_hi_ready, 1)
                pool.wait_ge(late_hi_ready, due(r, GROUPS, g + 1))
                nc.gpsimd.tensor_tensor(late_lo[:], whole, late_hi[:].bitcast(F32), ALU.subtract) \
                    .then_inc(late_lo_ready, 1)

            def split_low_u(r, n):
                b = n % 2
                pool.wait_ge(u_hi_ready, due(r, BATCHES, n + 1))
                if n >= 2:
                    pool.wait_ge(u_lo_ready, due(r, BATCHES, n))
                own_turn(pool, r, pool_turn)
                nc.gpsimd.tensor_scalar(u_sb[:], hT[:], a_sb[:, 0:1], 0.0, ALU.mult, ALU.add).then_inc(u_ready, 1)
                pool.wait_ge(u_ready, due(r, BATCHES, n))
                nc.gpsimd.tensor_tensor(u_lo[:, b], u_sb[:], u_hi[:, b].bitcast(F32), ALU.subtract) \
                    .then_inc(u_lo_ready, 1)

            def split_x(r, n):
                b = n % 2
                pool.wait_ge(x_loaded[b], due(r, 16, 16 * (n // 2 + 1)))
                if n >= 2:
                    pool.wait_ge(mix_step, due(r, PERIOD, TB * (n - 1)))
                own_turn(pool, r, pool_turn)
                nc.gpsimd.tensor_scalar(x_hi[:, b], x_sb[:, b, LATE:], 1.0, 0.0, ALU.mult, ALU.add).then_inc(x_hi_ready, 1)
                pool.wait_ge(x_hi_ready, due(r, BATCHES, n + 1))
                nc.gpsimd.tensor_tensor(x_lo[:, b], x_sb[:, b, LATE:], x_hi[:, b].bitcast(F32), ALU.subtract) \
                    .then_inc(x_lo_ready, 1)

            def find_rstd(r, g, nth, k):
                b = g % 2
                pool.wait_ge(moments_ready, due(r, PERIOD, G * g + k.stop))
                if g >= 1:
                    pool.wait_ge(normed_ready, due(r, GROUPS, g if g < LAST_G - 1 else g - 1))
                own_turn(pool, r, pool_turn)
                nc.gpsimd.tensor_scalar(negmean[:, b, k], moments[:, b, k, 0], -1.0, 0.0, ALU.mult, ALU.add) \
                    .then_inc(norm_step, 1)
                nc.gpsimd.tensor_scalar(rstd[:, b, k], moments[:, b, k, 1], EPS, 1.0, ALU.add, ALU.mult) \
                    .then_inc(norm_step, 1)
                pool.wait_ge(norm_step, due(r, 3 * GROUPS, 3 * nth + 2))
                nc.gpsimd.tensor_tensor(rstd[:, b, k], rstd[:, b, k], minus_half[:, k], ALU.pow).then_inc(norm_step, 1)

            def norm(r, g):
                b = g % 2
                find_rstd(r, g, g, slice(0, G))
                pool.wait_ge(norm_step, due(r, 3 * GROUPS, 3 * g + 3))
                if g >= 1:
                    pool.wait_ge(stored, due(r, 16 * GROUPS, 16 * g))
                own_turn(pool, r, pool_turn)
                for k in range(G):
                    ins = nc.gpsimd.tensor_scalar(normed[:, 0, k], y[:, b, k], negmean[:, b, k:k + 1],
                                                  rstd[:, b, k:k + 1], ALU.add, ALU.mult)
                ins.then_inc(normed_ready, 1)

            pool.wait_ge(a_loaded, 16)
            pool.wait_ge(hT_ready, 1)
            nc.gpsimd.tensor_scalar(u_hi[:, 0, 0:P], hT[:, 0:P], a_sb[:, 0:1], 0.0, ALU.mult, ALU.add) \
                .then_inc(first_u_hi_ready, 1)
            pool.wait_ge(hT_ready, 2)
            nc.gpsimd.tensor_scalar(u_hi[:, 0, P:], hT[:, P:], a_sb[:, 0:1], 0.0, ALU.mult, ALU.add) \
                .then_inc(u_hi_ready, 1)
            make_mask(0, 0)
            make_mask(0, 1)

            def step(r, s):
                n = s // TB + 1
                if s + 2 < T:
                    make_mask(r, s + 2)
                if n < B and s % TB == 2:
                    split_high_u(r, n)
                if n < B and s % TB == 4:
                    split_low_h(r, n)
                if s < T and s % TB == 5:
                    split_x(r, s // TB)
                if n < B and s % TB == 3:
                    split_low_u(r, n)
                g, at = divmod(s - MIX, G)
                if at == 0 and 0 <= g < LAST_G:
                    split_late(r, g)
                if (s - NORM) % G == 0 and s >= NORM and (s - NORM) // G < LAST_G - 1:
                    norm(r, (s - NORM) // G)

            steps(pool, step)
            find_rstd(0, LAST_G - 1, LAST_G - 1, slice(0, G))
            find_rstd(0, LAST_G, LAST_G, slice(0, 2))
            find_rstd(0, LAST_G, LAST_G + 1, slice(2, G))

            def tile(n):
                pool.wait_ge(g_moments_ready, n + 1)
                pool.wait_ge(g_done, n + 1)
                pool.sem_inc(g_turn["pool"], 1)
                nc.gpsimd.tensor_scalar(negmean[:, 0, 0:1], moments[:, 0, 0, 0:1], -1.0, 0.0, ALU.mult, ALU.add) \
                    .then_inc(g_norm_step, 1)
                nc.gpsimd.tensor_scalar(rstd[:, 0, 0:1], moments[:, 0, 0, 1:2], EPS, 1.0, ALU.add, ALU.mult) \
                    .then_inc(g_norm_step, 1)
                pool.wait_ge(g_norm_step, n * 3 + 2)
                nc.gpsimd.tensor_tensor(rstd[:, 0, 0:1], rstd[:, 0, 0:1], minus_half[:, 0:1], ALU.pow) \
                    .then_inc(g_norm_step, 1)
                pool.wait_ge(g_norm_step, n * 3 + 3)
                pool.sem_inc(g_turn["pool"], 1)
                nc.gpsimd.tensor_scalar(normed[:, 0, 0], y[:, 0, 0], negmean[:, 0, 0:1], rstd[:, 0, 0:1],
                                        ALU.add, ALU.mult).then_inc(g_normed_ready, 1)

            general(pool, None, tile)

        @block.tensor
        def _(pe):
            def keep_busy(count):
                for _ in range(count):
                    nc.tensor.transpose(mix[:, 0:P], ident[:], ident[:])

            def turn_x(r, s, n, half):
                if n == 0:
                    pe.wait_ge(x_first_loaded[half], 16)
                elif half == 0:
                    pe.wait_ge(x_turn_loaded, due(r, 16 * BATCHES, 16 * n))
                if s > TURN:
                    pe.wait_ge(probsT_lo_ready, due(r, PERIOD, s - TURN))
                bank = half if n <= 1 else 1
                for k in range(G):
                    mm = nc.tensor.transpose(turned[:, bank, k * P:(k + 1) * P], x_turn[:, half * G + k, :], ident[:])
                mm.then_inc(xT_ready, 1)

            def scores(r, t):
                J, b, slot = t % TB, t // TB % 2, t % 2
                if t == 0:
                    pe.wait_ge(first_u_lo_ready, 1)
                elif t == 1:
                    pe.wait_ge(u_lo_ready, 1)
                elif J == 0:
                    pe.wait_ge(h_lo_ready, due(r, BATCHES, t // TB + 1))
                    pe.wait_ge(u_lo_ready, due(r, BATCHES, t // TB + 1))
                if t >= 2:
                    pe.wait_ge(leaky_ready, due(r, PERIOD, t - 1))
                    if (t - 2) % TB:
                        pe.wait_ge(old_masked, due(r, OLD * BATCHES, OLD * ((t - 2) // TB) + (t - 2) % TB))
                pieces = [(max(J * P, c), c + HALF) for c in (0, HALF) if J * P < c + HALF]
                rows = slice(J * P, (J + 1) * P)
                for n, (u, h) in enumerate([(u_lo, h_hi), (u_hi, h_lo), (u_hi, h_hi)]):
                    if t == 0 and n == 1:
                        pe.wait_ge(h_lo_ready, 1)
                    for c0, c1 in pieces:
                        mm = nc.tensor.matmul(S[:, slot, c0:c1], u[:, b, rows], h[:, b, c0:c1],
                                              start=(n == 0), stop=(n == 2))
                for K in range(J):
                    if K == J - 1:
                        if t == 1:
                            keep_busy(9)
                        pe.wait_ge(leaky_ready, due(r, PERIOD, t))
                    mm = nc.tensor.transpose(S[:, slot, K * P:(K + 1) * P],
                                             leaky_cols(K, J * P, (J + 1) * P), ident[:])
                mm.then_inc(S_ready, 1)

            def turn(r, t, half):
                if half == 0:
                    pe.wait_ge(probs_ready, due(r, PERIOD, t + 1))
                else:
                    for n, x_half in x_turned_in(t + TURN):
                        pe.wait_ge(hT_ready, due(r, 2 * BATCHES, 2 * n + 1 + x_half))
                if t == 0:
                    pe.wait_ge(hT_ready, 3 + half)
                if t >= 1:
                    pe.wait_ge(probsT_lo_ready if half else probsT_ready, due(r, PERIOD, t))
                for k in range(G):
                    j = half * G + k
                    mm = nc.tensor.transpose(turned[:, half, k * P:(k + 1) * P],
                                             probs[:, t % 2, j * P:(j + 1) * P], ident[:])
                mm.then_inc(turned_ready, 1)

            def mix_block(r, g, i):
                if i == 0:
                    pe.wait_ge(probsT_ready, due(r, PERIOD, G * (g + 1)))
                    pe.wait_ge(x_loaded[g // 2 % 2], due(r, 16, 16 * (g // 4 + 1)))
                    if g >= 1:
                        pe.wait_ge(mixT_ready, due(r, GROUPS, g))
                j = MIX_ORDER[i]
                if j == G:
                    pe.wait_ge(probsT_lo_ready, due(r, PERIOD, G * (g + 1)))
                    pe.wait_ge(x_lo_ready, due(r, BATCHES, g // 2 + 1))
                if j == LATE:
                    pe.wait_ge(late_lo_ready, due(r, GROUPS, g + 1))
                    mm = mix_parts(mix[:], g // 2 % 2, j, late_hi[:], late_lo[:], last=True)
                else:
                    mm = mix_into(mix[:], g, j, slice(0, HALF))
                if i % 2:
                    mm.then_inc(mix_step, 1)

            def mix_into(to, g, j, rows, last=False):
                b = g // 2 % 2
                if j < G:
                    return nc.tensor.matmul(to, x_sb[:, b, j], probsT[:, g % 2, j, rows], start=(j == 0), stop=False)
                return mix_parts(to, b, j, probsT_hi[:, g % 2, j - G, rows], probsT_lo[:, g % 2, j - G, rows], last)

            def mix_parts(to, b, j, hi, lo, last):
                x_high, x_low = x_hi[:, b, j - LATE], x_lo[:, b, j - LATE]
                nc.tensor.matmul(to, x_low, hi, start=False, stop=False)
                nc.tensor.matmul(to, x_high, lo, start=False, stop=False)
                return nc.tensor.matmul(to, x_high, hi, start=False, stop=last)

            def mix_pair(pair, blocks):
                for j in blocks:
                    if j == 0:
                        pe.wait_ge(probsT_ready, G * LAST_G + 2 * pair + 2)
                    if j == G:
                        pe.wait_ge(probsT_lo_ready, G * LAST_G + 2 * pair + 2)
                    mm = mix_into(S[:, 0, pair * HALF:pair * HALF + PAIR], LAST_G, j,
                                  slice(pair * PAIR, (pair + 1) * PAIR), last=(j == TB - 1))
                if j == TB - 1:
                    mm.then_inc(last_mixed, 1)

            def back_pair(pair):
                pe.wait_ge(last_mixT_ready, pair + 1)
                for k in range(2):
                    mm = nc.tensor.transpose(S[:, 1, pair * HALF + k * P:pair * HALF + (k + 1) * P],
                                             last_mixT[:, (2 * pair + k) * P:(2 * pair + k + 1) * P], ident[:])
                mm.then_inc(last_back_ready, 1)

            def back(r, g):
                pe.wait_ge(mixT_ready, due(r, GROUPS, g + 1))
                if g >= 1:
                    pe.wait_ge(y_ready, due(r, PERIOD, G * g))
                for k in range(G):
                    mm = nc.tensor.transpose(aux[:, k * P:(k + 1) * P], mixT[:, k * P:(k + 1) * P], ident[:])
                mm.then_inc(back_ready, 1)

            pe.wait_ge(consts_ready, 1)
            keep_busy(9)
            turn_x(0, 0, 0, 0)
            turn_x(0, 0, 0, 1)
            keep_busy(12)

            def step(r, s):
                if s < T:
                    scores(r, s)
                if s == 1:
                    keep_busy(9)
                g, at = divmod(s - BACK, G)
                if at == 0 and 0 <= g < LAST_G - 1:
                    back(r, g)
                if 0 <= s - TURN < T:
                    turn(r, s - TURN, 0)
                g, q = divmod(s - MIX, G)
                if 0 <= g < LAST_G:
                    mix_block(r, g, 2 * q)
                for n, half in x_turned_in(s):
                    turn_x(r, s, n, half)
                if 0 <= s - TURN < T and s == T + 1:
                    turn(r, s - TURN, 1)
                if 0 <= g < LAST_G:
                    mix_block(r, g, 2 * q + 1)
                if 0 <= s - TURN < T and s != T + 1:
                    turn(r, s - TURN, 1)

            steps(pe, step)
            mix_pair(0, range(TB))
            back(0, LAST_G - 1)
            mix_pair(1, range(G))
            back_pair(0)
            mix_pair(1, range(G, TB))
            back_pair(1)

            pe.wait_ge(odd_ready, 1)
            nc.tensor.matmul(aux[0:1, 0:1], odd_rows[:], ones[:], start=True, stop=True).then_inc(counted, 1)

            def turn_batch(b):
                pe.wait_ge(g_x_loaded, b * 16 + 16)
                for half in range(2):
                    if half:
                        pe.wait_ge(g_hT_ready, b * 2 + 1)
                    for k in range(G):
                        mm = nc.tensor.transpose(aux[:, k * P:(k + 1) * P], x_sb[:, 0, half * G + k], ident[:])
                    mm.then_inc(g_xT_ready, 1)
                pe.wait_ge(g_hT_ready, b * 2 + 2)
                pe.sem_inc(g_turn["pe"], 1)

            def tile(n):
                pe.wait_ge(g_loaded, n * 32 + 32)
                nc.tensor.transpose(turned[:, 0, 0:P], g_rows, ident[:]).then_inc(g_rowsT_ready, 1)
                pe.wait_ge(g_u_ready, n + 1)
                for k in range(R):
                    if k >= 2:
                        pe.wait_ge(g_cand_ready, n * R + k - 1)
                    for c in (0, HALF):
                        mm = nc.tensor.matmul(S[:, k % 2, c:c + HALF], g_u[:, k], hT[:, c:c + HALF],
                                              start=True, stop=True)
                    mm.then_inc(g_S_ready, 1)
                pe.wait_ge(g_probs_ready, n + 1)
                for j in range(TB):
                    mm = nc.tensor.transpose(turned[:, j // G, j % G * P:(j % G + 1) * P],
                                             probs[:, 1, j * P:(j + 1) * P], ident[:])
                mm.then_inc(g_turned_ready, 1)
                pe.wait_ge(g_probsT_ready, n + 1)
                for j in range(TB):
                    mm = nc.tensor.matmul(mix[:, 0:D], g_probsT[:, j], x_sb[:, 0, j], start=(j == 0), stop=(j == TB - 1))
                mm.then_inc(g_mixed, 1)

            general(pe, turn_batch, tile)

        @block.scalar
        def _(act):
            act.wait_ge(consts_ready, 1)
            nc.scalar.activation(warm[:], ident[:, 0:1], ACT.Exp)

            def copy_x(r, n, half):
                act.wait_ge(xT_ready, due(r, 2 * BATCHES, 2 * n + 1 + half))
                if half == 0 and n >= 1:
                    act.wait_ge(h_lo_ready, due(r, BATCHES, n))
                    act.wait_ge(u_lo_ready, due(r, BATCHES, n))
                nc.scalar.copy(hT[:, half * HALF:(half + 1) * HALF], turned[:, half if n <= 1 else 1]) \
                    .then_inc(hT_ready, 1)

            def split_high_h(r, n):
                act.wait_ge(hT_ready, due(r, 2 * BATCHES, 2 * n + 2))
                nc.scalar.copy(h_hi[:, n % 2], hT[:]).then_inc(h_hi_ready, 1)

            def copy_scores(r, t):
                J = t % TB
                act.wait_ge(S_ready, due(r, PERIOD, t + 1))
                nc.scalar.copy(leaky_cols(J, J * P, N), S[:, t % 2, J * P:N]).then_inc(copied, 1)

            def exp(r, t):
                act.wait_ge(masked_ready, due(r, PERIOD, t + 1))
                if t >= 2:
                    act.wait_ge(turned_ready, due(r, 2 * PERIOD, 2 * (t - 1)))
                c = t % PERIOD
                nc.scalar.activation(probs[:, t % 2], masked[:, t % 2], ACT.Exp, bias=negmax[:, c:c + 1],
                                     scale=-1.0, accum_out=rowsum[:, c:c + 1]).then_inc(probs_ready, 1)

            def copy_turned(r, t, half):
                g, k = t // G, t % G
                act.wait_ge(turned_ready, due(r, 2 * PERIOD, 2 * t + 1 + half))
                if g >= 2 and k == 0 and half == 0:
                    act.wait_ge(mix_step, due(r, PERIOD, G * (g - 1)))
                to, done = ((probsT, probsT_ready), (probsT_hi, probsT_hi_ready))[half]
                nc.scalar.copy(to[:, g % 2, :, k * P:(k + 1) * P],
                               turned[:, half].rearrange("p (j i) -> p j i", j=G)).then_inc(done, 1)

            def copy_mix(r, g):
                act.wait_ge(mix_step, due(r, PERIOD, G * (g + 1)))
                if g >= 1:
                    act.wait_ge(back_ready, due(r, GROUPS, g))
                nc.scalar.copy(mixT[:], mix[:]).then_inc(mixT_ready, 1)

            def copy_pair(pair):
                act.wait_ge(last_mixed, pair + 1)
                act.wait_ge(probs_ready, T - 1)
                nc.scalar.copy(last_mixT[:, pair * PAIR:(pair + 1) * PAIR], S[:, 0, pair * HALF:pair * HALF + PAIR]) \
                    .then_inc(last_mixT_ready, 1)

            copy_x(0, 0, 0)
            copy_x(0, 0, 1)

            def step(r, s):
                if s < T:
                    copy_scores(r, s)
                if 0 <= s - 1 < T:
                    exp(r, s - 1)
                for n, half in x_turned_in(s):
                    copy_x(r, n, half)
                if s % TB == 3 and s // TB + 1 < B:
                    split_high_h(r, s // TB + 1)
                if 0 <= s - TURN < T:
                    copy_turned(r, s - TURN, 0)
                g, at = divmod(s - MIX - G + 1, G)
                if at == 0 and 0 <= g < LAST_G:
                    copy_mix(r, g)
                if 0 <= s - TURN < T:
                    copy_turned(r, s - TURN, 1)

            steps(act, step)
            copy_pair(0)
            copy_pair(1)

            def copy_batch(b):
                for half in range(2):
                    act.wait_ge(g_xT_ready, b * 2 + 1 + half)
                    nc.scalar.copy(hT[:, half * HALF:(half + 1) * HALF], aux[:]).then_inc(g_hT_ready, 1)

            def tile(n):
                act.wait_ge(g_max_ready, n + 1)
                nc.scalar.activation(probs[:, 1], g_best, ACT.Exp, bias=negmax[:, 0:1],
                                     accum_out=rowsum[:, 0:1]).then_inc(g_probs_ready, 1)
                act.wait_ge(g_turned_ready, n + 1)
                nc.scalar.copy(g_probsT, turned[:].rearrange("p h (j i) -> p (h j) i", j=G)).then_inc(g_probsT_ready, 1)

            general(act, copy_batch, tile)

        @block.vector
        def _(dve):
            def leak(r, t):
                J = t % TB
                kept = leaky_cols(J, J * P, N)
                dve.wait_ge(copied, due(r, PERIOD, t + 1))
                nc.vector.scalar_tensor_tensor(out=kept, in0=S[:, t % 2, J * P:N], scalar=SLOPE, in1=kept,
                                               op0=ALU.mult, op1=ALU.max).then_inc(leaky_ready, 1)

            def mask_old(r, t):
                J, slot = t % TB, t % 2
                dve.wait_ge(mask_ready, due(r, PERIOD, t + 1))
                if t >= 2:
                    dve.wait_ge(probs_ready, due(r, PERIOD, t - 1))
                own_turn(dve, r, dve_turn)
                if J:
                    old = slice(0, J * P)
                    nc.vector.tensor_tensor_reduce(masked[:, slot, old], S[:, slot, old], mask[:, t % RA, old],
                                                   -1.0, 3e38, ALU.add, ALU.min, oldmin[:, slot:slot + 1]) \
                        .then_inc(old_masked, 1)

            def mask_new(r, t):
                J, slot, c = t % TB, t % 2, t % PERIOD
                new = slice(J * P, N)
                dve.wait_ge(leaky_ready, due(r, PERIOD, t + 1))
                if J:
                    dve.wait_ge(old_masked, due(r, OLD * BATCHES, OLD * (t // TB) + J))
                own_turn(dve, r, dve_turn)
                nc.vector.tensor_tensor_reduce(masked[:, slot, new], leaky_cols(J, J * P, N), mask[:, t % RA, new],
                                               -1.0, oldmin[:, slot:slot + 1] if J else 3e38,
                                               ALU.add, ALU.min, negmax[:, c:c + 1]).then_inc(masked_ready, 1)

            def invert(r, g):
                c = g * G % PERIOD
                if g >= 1:
                    dve.wait_ge(y_ready, due(r, PERIOD, G * g))
                dve.wait_ge(probs_ready, due(r, PERIOD, G * (g + 1)))
                nc.vector.reciprocal(rinv[:], rowsum[:, c:c + G]).then_inc(rinv_ready, 1)

            def residual(r, t):
                g, k = divmod(t, G)
                came_back = aux[:, k * P:(k + 1) * P]
                if k == 0:
                    dve.wait_ge(rinv_ready, due(r, GROUPS, g + 1))
                    if g < LAST_G:
                        dve.wait_ge(back_ready, due(r, GROUPS, g + 1))
                    if g >= 2:
                        dve.wait_ge(normed_ready, due(r, GROUPS, g - 1))
                if g == LAST_G:
                    dve.wait_ge(last_back_ready, k // 2 + 1)
                    came_back = S[:, 1, k // 2 * HALF + k % 2 * P:k // 2 * HALF + (k % 2 + 1) * P]
                nc.vector.scalar_tensor_tensor(out=y[:, g % 2, k], in0=came_back,
                                               scalar=rinv[:, k:k + 1], in1=x_sb[:, t // TB % 2, t % TB],
                                               op0=ALU.mult, op1=ALU.add).then_inc(y_ready, 1)

            def gather_stats(r, t):
                g, k = divmod(t, G)
                dve.wait_ge(y_ready, due(r, PERIOD, t + 1))
                nc.vector.bn_stats(stats[:, k], y[:, g % 2, k]).then_inc(stats_ready, 1)

            def find_moments(r, t):
                g, k = divmod(t, G)
                dve.wait_ge(stats_ready, due(r, PERIOD, t + 1))
                own_turn(dve, r, dve_turn)
                nc.vector.bn_aggr(moments[:, g % 2, k], stats[:, k]).then_inc(moments_ready, 1)

            def check_batch(r, n):
                c = n * TB % PERIOD
                most, sums = negmax[:, c:c + TB], rowsum[:, c:c + TB]
                nc.vector.tensor_scalar(lifted[:], most, -BIG / 2, None, ALU.is_lt)
                nc.vector.tensor_scalar(uniform[:], sums, float(N), None, ALU.is_equal).then_inc(odd_step, 1)
                dve.wait_ge(odd_step, due(r, 4 * BATCHES, 4 * n + 1))
                nc.vector.scalar_tensor_tensor(out=uneven[:], in0=most, scalar=BIG / 2, in1=uniform[:],
                                               op0=ALU.is_gt, op1=ALU.is_gt).then_inc(odd_step, 1)
                dve.wait_ge(odd_step, due(r, 4 * BATCHES, 4 * n + 2))
                nc.vector.tensor_tensor(odd[:], odd[:], lifted[:], ALU.max).then_inc(odd_step, 1)
                dve.wait_ge(odd_step, due(r, 4 * BATCHES, 4 * n + 3))
                nc.vector.tensor_tensor(odd[:], odd[:], uneven[:], ALU.max).then_inc(odd_step, 1)

            def low_u(b, cols):
                return nc.vector.scalar_tensor_tensor(out=u_lo[:, b, cols], in0=hT[:, cols], scalar=a_sb[:, 0:1],
                                                      in1=u_hi[:, b, cols].bitcast(F32), op0=ALU.mult, op1=ALU.subtract)

            def split_low_probs(r, t):
                g, k = t // G, t % G
                dve.wait_ge(probsT_hi_ready, due(r, PERIOD, t + 1))
                if g >= 2 and k == 0:
                    dve.wait_ge(mix_step, due(r, PERIOD, G * (g - 1)))
                own_turn(dve, r, dve_turn)
                i = slice(k * P, (k + 1) * P)
                nc.vector.tensor_tensor(probsT_lo[:, g % 2, :, i], turned[:, 1].rearrange("p (j i) -> p j i", j=G),
                                        probsT_hi[:, g % 2, :, i].bitcast(F32), ALU.subtract) \
                    .then_inc(probsT_lo_ready, 1)

            left, right = slice(0, HALF), slice(HALF, N)
            dve.wait_ge(hT_ready, 1)
            nc.vector.tensor_copy(h_hi[:, 0, left], hT[:, left]).then_inc(first_part, 1)
            dve.wait_ge(hT_ready, 2)
            nc.vector.tensor_copy(h_hi[:, 0, right], hT[:, right]).then_inc(h_hi_ready, 1)
            dve.wait_ge(a_loaded, 16)
            dve.wait_ge(first_u_hi_ready, 1)
            low_u(0, slice(0, P)).then_inc(first_u_lo_ready, 1)
            dve.wait_ge(first_part, 1)
            nc.vector.tensor_tensor(h_lo[:, 0, left], hT[:, left], h_hi[:, 0, left].bitcast(F32), ALU.subtract)
            dve.wait_ge(h_hi_ready, 1)
            nc.vector.tensor_tensor(h_lo[:, 0, right], hT[:, right], h_hi[:, 0, right].bitcast(F32), ALU.subtract) \
                .then_inc(h_lo_ready, 1)
            dve.wait_ge(u_hi_ready, 1)
            low_u(0, slice(P, N)).then_inc(u_lo_ready, 1)

            def step(r, s):
                rest = s - REST if 0 <= s - REST < G * (LAST_G - 1) else None
                if s < T:
                    leak(r, s)
                if rest is not None and rest % G == 0:
                    invert(r, rest // G)
                if rest is not None:
                    residual(r, rest)
                if s < T:
                    mask_old(r, s)
                if rest is not None:
                    gather_stats(r, rest)
                if s < T:
                    mask_new(r, s)
                if 0 <= s - TURN < T:
                    split_low_probs(r, s - TURN)
                if rest is not None:
                    find_moments(r, rest)
                if s % TB == 2 and TB < s < T + TB:
                    dve.wait_ge(probs_ready, due(r, PERIOD, s - 2))
                    check_batch(r, s // TB - 1)

            steps(dve, step)

            def finish(tiles):
                for stage in (residual, gather_stats, find_moments):
                    for t in tiles:
                        stage(0, t)

            def norm_last(g, nth, tiles):
                dve.wait_ge(norm_step, 3 * nth + 3)
                slot = 0 if g == LAST_G else 1
                if g == LAST_G:
                    dve.wait_ge(stored, 16 * (LAST_G - 1))
                for k in tiles:
                    ins = nc.vector.tensor_scalar(normed[:, slot, k], y[:, g % 2, k], negmean[:, g % 2, k:k + 1],
                                                  rstd[:, g % 2, k:k + 1], ALU.add, ALU.mult)
                ins.then_inc(normed_ready, 1)

            last = G * LAST_G
            invert(0, LAST_G - 1)
            finish(range(last - G, last))
            invert(0, LAST_G)
            for pair in range(2):
                finish(range(last + 2 * pair, last + 2 * pair + 2))
            norm_last(LAST_G - 1, LAST_G - 1, range(G))
            norm_last(LAST_G, LAST_G, range(2))
            norm_last(LAST_G, LAST_G + 1, range(2, G))

            dve.wait_ge(a_rest_loaded, 48)
            dve.wait_ge(odd_step, 4 * B)
            nc.vector.reduce_max(odd_rows[:], odd[:], AX.X).then_inc(odd_ready, 1)
            dve.wait_ge(counted, 1)
            nc.vector.tensor_copy(verdict[:], aux[0:1, 0:1]).then_inc(verdict_ready, 1)

            def tile(n):
                dve.wait_ge(g_rowsT_ready, n + 1)
                for k in range(R):
                    ins = nc.vector.tensor_scalar(g_u[:, k], turned[:, 0, 0:P], a_sb[:, k:k + 1],
                                                  None, ALU.mult)
                ins.then_inc(g_u_ready, 1)
                for k in range(R):
                    if k:
                        dve.wait_ge(g_cand_ready, n * R + k)
                    nc.vector.tensor_scalar(g_mask, adj_sb[:, 0], float(k + 1), -1.0, ALU.is_equal, ALU.add) \
                        .then_inc(g_edges_ready, 1)
                    dve.wait_ge(g_edges_ready, n * R + k + 1)
                    dve.wait_ge(g_S_ready, n * R + k + 1)
                    if k >= 2:
                        dve.wait_ge(g_best_ready, n * (R - 1) + k - 1)
                    nc.vector.scalar_tensor_tensor(out=masked[:, 0] if k else g_best, in0=g_mask, scalar=BIG,
                                                   in1=S[:, k % 2], op0=ALU.mult, op1=ALU.add).then_inc(g_cand_ready, 1)
                    if k:
                        dve.wait_ge(g_cand_ready, n * R + k + 1)
                        nc.vector.tensor_tensor(g_best, g_best, masked[:, 0], ALU.max).then_inc(g_best_ready, 1)
                dve.wait_ge(g_best_ready, n * (R - 1) + R - 1)
                nc.vector.scalar_tensor_tensor(out=g_best, in0=g_best, scalar=SLOPE, in1=g_best,
                                               op0=ALU.mult, op1=ALU.max).then_inc(g_leaky_ready, 1)
                dve.wait_ge(g_leaky_ready, n + 1)
                nc.vector.tensor_reduce(negmax[:, 0:1], g_best, AX.X, ALU.max, negate=True).then_inc(g_max_ready, 1)
                dve.wait_ge(g_mixed, n + 1)
                nc.vector.reciprocal(rinv[:, 0:1], rowsum[:, 0:1]).then_inc(g_rinv_ready, 1)
                dve.wait_ge(g_rinv_ready, n + 1)
                nc.vector.scalar_tensor_tensor(out=y[:, 0, 0], in0=mix[:, 0:D], scalar=rinv[:, 0:1], in1=g_rows,
                                               op0=ALU.mult, op1=ALU.add).then_inc(g_y_ready, 1)
                dve.wait_ge(g_y_ready, n + 1)
                nc.vector.bn_stats(stats[:, 0], y[:, 0, 0]).then_inc(g_stats_ready, 1)
                dve.wait_ge(g_stats_ready, n + 1)
                dve.sem_inc(g_turn["dve"], 1)
                nc.vector.bn_aggr(moments[:, 0, 0], stats[:, 0]).then_inc(g_moments_ready, 1)

            general(dve, None, tile)


_INS=['x','adj','L0_gnn_a_0','L0_gnn_a_1','L0_gnn_a_2','L0_gnn_a_3']
def kernel(**inputs):
    import numpy as _np
    import concourse.bacc as _bacc
    from concourse import mybir as _mybir
    from concourse.bass_utils import run_bass_kernel_spmd as _run
    nc = _bacc.Bacc("TRN2", target_bir_lowering=False, num_devices=1)
    arrays, args = {}, []
    for name in _INS:
        a = _np.ascontiguousarray(inputs[name])
        arrays[f"in_{name}_dram"] = a
        args.append(nc.dram_tensor(f"in_{name}_dram", a.shape, _mybir.dt.from_np(a.dtype), kind="ExternalInput").ap())
    args.append(nc.dram_tensor("out_0_dram", (8,1024,128), _mybir.dt.float32, kind="ExternalOutput").ap())
    gat_residual_norm(nc, *args)
    r = _run(nc, [arrays], core_ids=[0])
    return r.results[0]["out_0_dram"]
```
